# Optimizing a Trainium2 kernel written in Bass

```python
import numpy as np
import jax
import jax.numpy as jnp

def _softmax(x, axis=-1):
    return jax.nn.softmax(x, axis=axis)

def _gelu(x):
    return jax.nn.gelu(x, approximate=True)

def _silu(x):
    return jax.nn.silu(x)

def _sigmoid(x):
    return jax.nn.sigmoid(x)

def _layernorm(x, axis=-1, eps=1e-05):
    m = jnp.mean(x, axis=axis, keepdims=True)
    v = jnp.var(x, axis=axis, keepdims=True)
    return (x - m) / jnp.sqrt(v + eps)

def _scatter_add(tgt, idx, src, axis=0):
    return tgt.at[idx].add(src)

def _segment_sum(src, seg, n):
    return jax.ops.segment_sum(src, seg, n)
kernel_name = 'mk_xattn_ffn_d4_seqx_r8_757089'

def setup_inputs(seed: int=0):
    np.random.seed(seed)
    _w = jnp.asarray

    def _rec_inputs():
        import jax
        import jax.numpy as jnp
        _rk = jax.random.key(seed)
        x = 7.22e-05 + 1 * jax.random.normal(jax.random.fold_in(_rk, 1), (32, 128, 128), jnp.float32)
        _lenS = 128 - jax.random.randint(jax.random.fold_in(_rk, 7), (32,), 0, max(1, 128 // 4) + 1, jnp.int32)
        _lenS2 = 128 - jax.random.randint(jax.random.fold_in(_rk, 8), (32,), 0, max(1, 128 // 4) + 1, jnp.int32)
        _ctx_1024P = jax.random.normal(jax.random.fold_in(_rk, 11), (32, 16, 128), jnp.float32)
        _ctx_1024c = jax.random.dirichlet(jax.random.fold_in(_rk, 511), 0.3 * jnp.ones((16,), jnp.float32), (32, 128))
        _ctx_1024t = jnp.einsum('bsk,bkd->bsd', _ctx_1024c, _ctx_1024P)
        _ctx_1024t = _ctx_1024t * jax.lax.rsqrt(jnp.mean(jnp.square(_ctx_1024t)) + 1e-12) * 0.953939
        ctx_1024 = 4.13588e-05 + 0.999923 * (_ctx_1024t + 0.3 * jax.random.normal(jax.random.fold_in(_rk, 611), (32, 128, 128), jnp.float32))
        return (x, ctx_1024)
    x, ctx_1024 = _rec_inputs()

    def _L0_xattn_setup():
        import jax, jax.numpy as jnp
        import numpy as np
        B, T, D, H = (4, 256, 128, 16)
        DK = D // H

        def _split_heads(x):
            b, t, _ = x.shape
            return x.reshape(b, t, H, DK).transpose(0, 2, 1, 3)
        key = jax.random.key(seed)
        ks = jax.random.split(key, 8)
        std = 1.0 / np.sqrt(2.0 * D)
        inp = {'q': jax.random.normal(ks[0], (B, T, D), jnp.float32), 'k': jax.random.normal(ks[1], (B, T, D), jnp.float32), 'v': jax.random.normal(ks[2], (B, T, D), jnp.float32), 'Wq': jax.random.normal(ks[3], (D, D), jnp.float32) * std, 'Wk': jax.random.normal(ks[4], (D, D), jnp.float32) * std, 'Wv': jax.random.normal(ks[5], (D, D), jnp.float32) * std, 'Wo': jax.random.normal(ks[6], (D, D), jnp.float32) * std, 'bq': jnp.zeros((D,), jnp.float32), 'bk': jnp.zeros((D,), jnp.float32), 'bv': jnp.zeros((D,), jnp.float32), 'bo': jnp.zeros((D,), jnp.float32)}
        return inp
    _L0_xattn_all = _L0_xattn_setup()
    _L0_xattn_in = {k: v for k, v in _L0_xattn_all.items() if k in ('Wq', 'Wk', 'Wv', 'Wo', 'bq', 'bk', 'bv', 'bo')}
    del _L0_xattn_all

    def _L0_ffn_setup():
        import jax, jax.numpy as jnp
        import numpy as np
        D_MODEL = 128
        NUM_EXPERTS = 8
        TOP_K = 2
        key = jax.random.key(seed)
        k_x, k_g, k_w1, k_w2 = jax.random.split(key, 4)
        B, S, D, E = (4, 256, D_MODEL, NUM_EXPERTS)
        s_in = 1.0 / np.sqrt(D)
        s_hid = 1.0 / np.sqrt(4 * D)
        return {'x': jax.random.normal(k_x, (B, S, D), dtype=jnp.float32), 'gate_w': jax.random.uniform(k_g, (E, D), jnp.float32, -s_in, s_in), 'w1': jax.random.uniform(k_w1, (E, 4 * D, D), jnp.float32, -s_in, s_in), 'w2': jax.random.uniform(k_w2, (E, D, 4 * D), jnp.float32, -s_hid, s_hid)}
    _L0_ffn_all = _L0_ffn_setup()
    _L0_ffn_in = {k: v for k, v in _L0_ffn_all.items() if k in ('gate_w', 'w1', 'w2')}
    del _L0_ffn_all

    def _L1_xattn_setup():
        import jax, jax.numpy as jnp
        import numpy as np
        B, S, D, H = (4, 256, 128, 16)
        HD = D // H
        key = jax.random.key(seed)
        ks = jax.random.split(key, 11)
        s = 1.0 / np.sqrt(D)
        return {'query': jax.random.normal(ks[0], (B, S, D), jnp.float32), 'key': jax.random.normal(ks[1], (B, S, D), jnp.float32), 'value': jax.random.normal(ks[2], (B, S, D), jnp.float32), 'Wq': jax.random.normal(ks[3], (D, D), jnp.float32) * s, 'bq': jnp.zeros((D,), jnp.float32), 'Wk': jax.random.normal(ks[4], (D, D), jnp.float32) * s, 'bk': jnp.zeros((D,), jnp.float32), 'Wv': jax.random.normal(ks[5], (D, D), jnp.float32) * s, 'bv': jnp.zeros((D,), jnp.float32), 'Wo': jax.random.normal(ks[6], (D, D), jnp.float32) * s, 'bo': jnp.zeros((D,), jnp.float32)}
    _L1_xattn_all = _L1_xattn_setup()
    _L1_xattn_in = {k: v for k, v in _L1_xattn_all.items() if k in ('Wq', 'bq', 'Wk', 'bk', 'Wv', 'bv', 'Wo', 'bo')}
    del _L1_xattn_all

    def _L1_ffn_setup():
        import jax, jax.numpy as jnp
        import numpy as np
        B, S, H, M, E, K = (4, 256, 128, 512, 8, 2)
        key = jax.random.key(seed)
        ks = jax.random.split(key, 6)
        x = jax.random.normal(ks[0], (B, S, H), dtype=jnp.float32)
        Wr = jax.random.normal(ks[1], (E, H), dtype=jnp.float32) * (1.0 / np.sqrt(H))
        W1 = jax.random.normal(ks[2], (E, M, H), dtype=jnp.float32) * np.sqrt(2.0 / (H + M))
        b1 = jax.random.normal(ks[3], (E, M), dtype=jnp.float32) * 1e-06
        W2 = jax.random.normal(ks[4], (E, H, M), dtype=jnp.float32) * np.sqrt(2.0 / (H + M))
        b2 = jax.random.normal(ks[5], (E, H), dtype=jnp.float32) * 1e-06
        return {'x': x, 'Wr': Wr, 'W1': W1, 'b1': b1, 'W2': W2, 'b2': b2}
    _L1_ffn_all = _L1_ffn_setup()
    _L1_ffn_in = {k: v for k, v in _L1_ffn_all.items() if k in ('Wr', 'W1', 'b1', 'W2', 'b2')}
    del _L1_ffn_all

    def _L2_xattn_setup():
        import jax, jax.numpy as jnp
        import numpy as np
        D_MODEL = 128
        N_HEADS = 16
        HEAD = D_MODEL // N_HEADS
        D_FF = 512
        LN_EPS = 1e-05

        def _layernorm(x, g, b):
            mu = jnp.mean(x, axis=-1, keepdims=True)
            var = jnp.mean(jnp.square(x - mu), axis=-1, keepdims=True)
            return (x - mu) * jax.lax.rsqrt(var + LN_EPS) * g + b

        def _mha(q_in, k_in, v_in, Wq, Wk, Wv, bv, causal):
            q = jnp.einsum('bsd,hde->bhse', q_in, Wq)
            k = jnp.einsum('btd,hde->bhte', k_in, Wk)
            v = jnp.einsum('btd,hde->bhte', v_in, Wv) + bv[None, :, None, :]
            scale = HEAD ** (-0.5)
            scores = jnp.einsum('bhse,bhte->bhst', q, k) * scale
            if causal:
                S, T = (scores.shape[-2], scores.shape[-1])
                mask = jnp.tril(jnp.ones((S, T), dtype=bool))
                scores = jnp.where(mask, scores, -jnp.inf)
            p = jax.nn.softmax(scores, axis=-1)
            o = jnp.einsum('bhst,bhte->bhse', p, v)
            B, H, S, E = o.shape
            return o.transpose(0, 2, 1, 3).reshape(B, S, H * E)
        key = jax.random.key(seed)
        ks = jax.random.split(key, 20)
        B, S, T = (2, 256, 256)
        sd = D_MODEL ** (-0.5)
        inp = {'input_tensor': jax.random.normal(ks[0], (B, S, D_MODEL), jnp.float32), 'encoder_output': jax.random.normal(ks[1], (B, T, D_MODEL), jnp.float32), 'Wq1': jax.random.normal(ks[2], (N_HEADS, D_MODEL, HEAD), jnp.float32) * sd, 'Wk1': jax.random.normal(ks[3], (N_HEADS, D_MODEL, HEAD), jnp.float32) * sd, 'Wv1': jax.random.normal(ks[4], (N_HEADS, D_MODEL, HEAD), jnp.float32) * sd, 'bv1': jnp.zeros((N_HEADS, HEAD), jnp.float32), 'Wq2': jax.random.normal(ks[5], (N_HEADS, D_MODEL, HEAD), jnp.float32) * sd, 'Wk2': jax.random.normal(ks[6], (N_HEADS, D_MODEL, HEAD), jnp.float32) * sd, 'Wv2': jax.random.normal(ks[7], (N_HEADS, D_MODEL, HEAD), jnp.float32) * sd, 'bv2': jnp.zeros((N_HEADS, HEAD), jnp.float32), 'g1': jnp.ones((D_MODEL,), jnp.float32), 'be1': jnp.zeros((D_MODEL,), jnp.float32), 'g2': jnp.ones((D_MODEL,), jnp.float32), 'be2': jnp.zeros((D_MODEL,), jnp.float32), 'g3': jnp.ones((D_MODEL,), jnp.float32), 'be3': jnp.zeros((D_MODEL,), jnp.float32), 'Wf1': jax.random.normal(ks[8], (D_MODEL, D_FF), jnp.float32) * sd, 'bf1': jnp.zeros((D_FF,), jnp.float32), 'Wf2': jax.random.normal(ks[9], (D_FF, D_MODEL), jnp.float32) * D_FF ** (-0.5), 'bf2': jnp.zeros((D_MODEL,), jnp.float32)}
        return inp
    _L2_xattn_all = _L2_xattn_setup()
    _L2_xattn_in = {k: v for k, v in _L2_xattn_all.items() if k in ('Wq1', 'Wk1', 'Wv1', 'bv1', 'Wq2', 'Wk2', 'Wv2', 'bv2', 'g1', 'be1', 'g2', 'be2', 'g3', 'be3', 'Wf1', 'bf1', 'Wf2', 'bf2')}
    del _L2_xattn_all

    def _L2_ffn_setup():
        import jax, jax.numpy as jnp
        import numpy as np
        H = 16
        TOP_K = 2
        LN_EPS = 1e-05
        key = jax.random.key(seed)
        ks = jax.random.split(key, 8)
        B, S, E, NE = (2, 128, 128, 8)
        w = lambda k, shp: jax.random.normal(k, shp, dtype=jnp.float32) * 0.02
        return {'x': jax.random.normal(ks[0], (B, S, E), dtype=jnp.float32), 'rW1': w(ks[1], (E // 2, E)), 'rb1': jnp.zeros((E // 2,), jnp.float32), 'ln_g': jnp.ones((E // 2,), jnp.float32), 'ln_b': jnp.zeros((E // 2,), jnp.float32), 'rW2': w(ks[2], (NE, E // 2)), 'rb2': jnp.zeros((NE,), jnp.float32), 'qW': w(ks[3], (NE, E, E)), 'qb': jnp.zeros((NE, E), jnp.float32), 'kW': w(ks[4], (NE, E, E)), 'kb': jnp.zeros((NE, E), jnp.float32), 'vW': w(ks[5], (NE, E, E)), 'vb': jnp.zeros((NE, E), jnp.float32), 'oW': w(ks[6], (NE, E, E)), 'ob': jnp.zeros((NE, E), jnp.float32)}
    _L2_ffn_all = _L2_ffn_setup()
    _L2_ffn_in = {k: v for k, v in _L2_ffn_all.items() if k in ('rW1', 'rb1', 'ln_g', 'ln_b', 'rW2', 'rb2', 'qW', 'qb', 'kW', 'kb', 'vW', 'vb', 'oW', 'ob')}
    del _L2_ffn_all

    def _L3_xattn_setup():
        import jax, jax.numpy as jnp
        import numpy as np
        EMBED_DIM = 128
        NUM_HEADS = 16
        HEAD_DIM = EMBED_DIM // NUM_HEADS
        WINDOW = 64

        def apply_rope(x):
            B, H, S, d = x.shape
            half = d // 2
            pos = jnp.arange(S, dtype=x.dtype)
            freqs = 1.0 / 10000.0 ** (jnp.arange(half, dtype=x.dtype) / half)
            ang = pos[:, None] * freqs[None, :]
            cos, sin = (jnp.cos(ang), jnp.sin(ang))
            x1, x2 = (x[..., :half], x[..., half:])
            return jnp.concatenate([x1 * cos - x2 * sin, x1 * sin + x2 * cos], axis=-1)

        def _forward(query, key, value, q_w, q_b, k_w, k_b, v_w, v_b, o_w, o_b):
            B, S_q, D = query.shape
            S_k = key.shape[1]
            H, d, W = (NUM_HEADS, HEAD_DIM, WINDOW)
            q = (query @ q_w.T + q_b).reshape(B, S_q, H, d).transpose(0, 2, 1, 3)
            k = (key @ k_w.T + k_b).reshape(B, S_k, H, d).transpose(0, 2, 1, 3)
            v = (value @ v_w.T + v_b).reshape(B, S_k, H, d).transpose(0, 2, 1, 3)
            q = apply_rope(q) * d ** (-0.5)
            k = apply_rope(k)
            q_pos = jnp.arange(S_q)[:, None]
            offsets = jnp.arange(-W, 1)[None, :]
            idx = q_pos + offsets
            local_mask = (idx < 0) | (idx >= S_k)
            gidx = jnp.clip(idx, 0, S_k - 1)
            k_win = k[:, :, gidx, :]
            v_win = v[:, :, gidx, :]
            scores = jnp.einsum('bhqd,bhqwd->bhqw', q, k_win)
            mask = local_mask[None, None, :, :]
            scores = jnp.where(mask, -jnp.inf, scores)
            m = jnp.max(scores, axis=-1, keepdims=True)
            m = jnp.where(jnp.isfinite(m), m, 0.0)
            e = jnp.exp(scores - m)
            denom = jnp.sum(e, axis=-1, keepdims=True)
            probs = jnp.where(denom > 0, e / jnp.where(denom > 0, denom, 1.0), 0.0)
            ctx = jnp.einsum('bhqw,bhqwd->bhqd', probs, v_win)
            ctx = ctx.transpose(0, 2, 1, 3).reshape(B, S_q, D)
            return ctx @ o_w.T + o_b
        key = jax.random.key(seed)
        ks = jax.random.split(key, 12)
        B, S, D = (1, 256, EMBED_DIM)
        scale = 1.0 / np.sqrt(D)
        inp = {'query': jax.random.normal(ks[0], (B, S, D), jnp.float32), 'key': jax.random.normal(ks[1], (B, S, D), jnp.float32), 'value': jax.random.normal(ks[2], (B, S, D), jnp.float32), 'q_w': jax.random.normal(ks[3], (D, D), jnp.float32) * scale, 'q_b': jax.random.normal(ks[4], (D,), jnp.float32) * 0.01, 'k_w': jax.random.normal(ks[5], (D, D), jnp.float32) * scale, 'k_b': jax.random.normal(ks[6], (D,), jnp.float32) * 0.01, 'v_w': jax.random.normal(ks[7], (D, D), jnp.float32) * scale, 'v_b': jax.random.normal(ks[8], (D,), jnp.float32) * 0.01, 'o_w': jax.random.normal(ks[9], (D, D), jnp.float32) * scale, 'o_b': jax.random.normal(ks[10], (D,), jnp.float32) * 0.01}
        return inp
    _L3_xattn_all = _L3_xattn_setup()
    _L3_xattn_in = {k: v for k, v in _L3_xattn_all.items() if k in ('q_w', 'q_b', 'k_w', 'k_b', 'v_w', 'v_b', 'o_w', 'o_b')}
    del _L3_xattn_all

    def _L3_ffn_setup():
        import jax, jax.numpy as jnp
        import numpy as np
        TOP_K = 2
        key = jax.random.key(seed)
        k1, k2, k3, k4, k5 = jax.random.split(key, 5)
        B, S, D, F, E = (2, 128, 128, 256, 8)
        return {'x': jax.random.normal(k1, (B, S, D), dtype=jnp.float32), 'router_kernel_DE': jax.random.normal(k2, (D, E), dtype=jnp.float32) * 0.02, 'kernel_gating_EDF': jax.random.normal(k3, (E, D, F), dtype=jnp.float32) * 0.02, 'kernel_up_EDF': jax.random.normal(k4, (E, D, F), dtype=jnp.float32) * 0.02, 'kernel_down_EFD': jax.random.normal(k5, (E, F, D), dtype=jnp.float32) * 0.02}
    _L3_ffn_all = _L3_ffn_setup()
    _L3_ffn_in = {k: v for k, v in _L3_ffn_all.items() if k in ('router_kernel_DE', 'kernel_gating_EDF', 'kernel_up_EDF', 'kernel_down_EFD')}
    del _L3_ffn_all
    return {'x': x, 'ctx_1024': ctx_1024, 'L0_xattn_Wq': _L0_xattn_in['Wq'], 'L0_xattn_Wk': _L0_xattn_in['Wk'], 'L0_xattn_Wv': _L0_xattn_in['Wv'], 'L0_xattn_Wo': _L0_xattn_in['Wo'], 'L0_xattn_bq': _L0_xattn_in['bq'], 'L0_xattn_bk': _L0_xattn_in['bk'], 'L0_xattn_bv': _L0_xattn_in['bv'], 'L0_xattn_bo': _L0_xattn_in['bo'], 'L0_ffn_gate_w': _L0_ffn_in['gate_w'], 'L0_ffn_w1': _L0_ffn_in['w1'], 'L0_ffn_w2': _L0_ffn_in['w2'], 'L1_xattn_Wq': _L1_xattn_in['Wq'], 'L1_xattn_bq': _L1_xattn_in['bq'], 'L1_xattn_Wk': _L1_xattn_in['Wk'], 'L1_xattn_bk': _L1_xattn_in['bk'], 'L1_xattn_Wv': _L1_xattn_in['Wv'], 'L1_xattn_bv': _L1_xattn_in['bv'], 'L1_xattn_Wo': _L1_xattn_in['Wo'], 'L1_xattn_bo': _L1_xattn_in['bo'], 'L1_ffn_Wr': _L1_ffn_in['Wr'], 'L1_ffn_W1': _L1_ffn_in['W1'], 'L1_ffn_b1': _L1_ffn_in['b1'], 'L1_ffn_W2': _L1_ffn_in['W2'], 'L1_ffn_b2': _L1_ffn_in['b2'], 'L2_xattn_Wq1': _L2_xattn_in['Wq1'], 'L2_xattn_Wk1': _L2_xattn_in['Wk1'], 'L2_xattn_Wv1': _L2_xattn_in['Wv1'], 'L2_xattn_bv1': _L2_xattn_in['bv1'], 'L2_xattn_Wq2': _L2_xattn_in['Wq2'], 'L2_xattn_Wk2': _L2_xattn_in['Wk2'], 'L2_xattn_Wv2': _L2_xattn_in['Wv2'], 'L2_xattn_bv2': _L2_xattn_in['bv2'], 'L2_xattn_g1': _L2_xattn_in['g1'], 'L2_xattn_be1': _L2_xattn_in['be1'], 'L2_xattn_g2': _L2_xattn_in['g2'], 'L2_xattn_be2': _L2_xattn_in['be2'], 'L2_xattn_g3': _L2_xattn_in['g3'], 'L2_xattn_be3': _L2_xattn_in['be3'], 'L2_xattn_Wf1': _L2_xattn_in['Wf1'], 'L2_xattn_bf1': _L2_xattn_in['bf1'], 'L2_xattn_Wf2': _L2_xattn_in['Wf2'], 'L2_xattn_bf2': _L2_xattn_in['bf2'], 'L2_ffn_rW1': _L2_ffn_in['rW1'], 'L2_ffn_rb1': _L2_ffn_in['rb1'], 'L2_ffn_ln_g': _L2_ffn_in['ln_g'], 'L2_ffn_ln_b': _L2_ffn_in['ln_b'], 'L2_ffn_rW2': _L2_ffn_in['rW2'], 'L2_ffn_rb2': _L2_ffn_in['rb2'], 'L2_ffn_qW': _L2_ffn_in['qW'], 'L2_ffn_qb': _L2_ffn_in['qb'], 'L2_ffn_kW': _L2_ffn_in['kW'], 'L2_ffn_kb': _L2_ffn_in['kb'], 'L2_ffn_vW': _L2_ffn_in['vW'], 'L2_ffn_vb': _L2_ffn_in['vb'], 'L2_ffn_oW': _L2_ffn_in['oW'], 'L2_ffn_ob': _L2_ffn_in['ob'], 'L3_xattn_q_w': _L3_xattn_in['q_w'], 'L3_xattn_q_b': _L3_xattn_in['q_b'], 'L3_xattn_k_w': _L3_xattn_in['k_w'], 'L3_xattn_k_b': _L3_xattn_in['k_b'], 'L3_xattn_v_w': _L3_xattn_in['v_w'], 'L3_xattn_v_b': _L3_xattn_in['v_b'], 'L3_xattn_o_w': _L3_xattn_in['o_w'], 'L3_xattn_o_b': _L3_xattn_in['o_b'], 'L3_ffn_router_kernel_DE': _L3_ffn_in['router_kernel_DE'], 'L3_ffn_kernel_gating_EDF': _L3_ffn_in['kernel_gating_EDF'], 'L3_ffn_kernel_up_EDF': _L3_ffn_in['kernel_up_EDF'], 'L3_ffn_kernel_down_EFD': _L3_ffn_in['kernel_down_EFD']}

def reference(x, ctx_1024, L0_xattn_Wq, L0_xattn_Wk, L0_xattn_Wv, L0_xattn_Wo, L0_xattn_bq, L0_xattn_bk, L0_xattn_bv, L0_xattn_bo, L0_ffn_gate_w, L0_ffn_w1, L0_ffn_w2, L1_xattn_Wq, L1_xattn_bq, L1_xattn_Wk, L1_xattn_bk, L1_xattn_Wv, L1_xattn_bv, L1_xattn_Wo, L1_xattn_bo, L1_ffn_Wr, L1_ffn_W1, L1_ffn_b1, L1_ffn_W2, L1_ffn_b2, L2_xattn_Wq1, L2_xattn_Wk1, L2_xattn_Wv1, L2_xattn_bv1, L2_xattn_Wq2, L2_xattn_Wk2, L2_xattn_Wv2, L2_xattn_bv2, L2_xattn_g1, L2_xattn_be1, L2_xattn_g2, L2_xattn_be2, L2_xattn_g3, L2_xattn_be3, L2_xattn_Wf1, L2_xattn_bf1, L2_xattn_Wf2, L2_xattn_bf2, L2_ffn_rW1, L2_ffn_rb1, L2_ffn_ln_g, L2_ffn_ln_b, L2_ffn_rW2, L2_ffn_rb2, L2_ffn_qW, L2_ffn_qb, L2_ffn_kW, L2_ffn_kb, L2_ffn_vW, L2_ffn_vb, L2_ffn_oW, L2_ffn_ob, L3_xattn_q_w, L3_xattn_q_b, L3_xattn_k_w, L3_xattn_k_b, L3_xattn_v_w, L3_xattn_v_b, L3_xattn_o_w, L3_xattn_o_b, L3_ffn_router_kernel_DE, L3_ffn_kernel_gating_EDF, L3_ffn_kernel_up_EDF, L3_ffn_kernel_down_EFD):
    import jax
    import jax.numpy as jnp

    def _L0_xattn_ref(q, k, v, Wq, Wk, Wv, Wo, bq, bk, bv, bo):
        import jax, jax.numpy as jnp
        import numpy as np
        B, T, D, H = (4, 256, 128, 16)
        DK = D // H

        def _split_heads(x):
            b, t, _ = x.shape
            return x.reshape(b, t, H, DK).transpose(0, 2, 1, 3)
        qh = _split_heads(q @ Wq.T + bq)
        kh = _split_heads(k @ Wk.T + bk)
        vh = _split_heads(v @ Wv.T + bv)
        scores = jnp.einsum('bhqd,bhkd->bhqk', qh, kh) / jnp.sqrt(jnp.float32(DK))
        tq, tk = (scores.shape[-2], scores.shape[-1])
        causal = jnp.tril(jnp.ones((tq, tk), dtype=bool))
        scores = jnp.where(causal, scores, jnp.float32(-jnp.inf))
        attn = jax.nn.softmax(scores, axis=-1)
        ctx = jnp.einsum('bhqk,bhkd->bhqd', attn, vh)
        merged = ctx.transpose(0, 2, 1, 3).reshape(q.shape[0], tq, D)
        return merged @ Wo.T + bo

    def _L0_ffn_ref(x, gate_w, w1, w2):
        import jax, jax.numpy as jnp
        import numpy as np
        D_MODEL = 128
        NUM_EXPERTS = 8
        TOP_K = 2
        gate_logits = jnp.einsum('bsd,ed->bse', x, gate_w)
        top_v, top_i = jax.lax.top_k(gate_logits, TOP_K)
        gates = jax.nn.softmax(top_v, axis=-1)
        combine = jnp.sum(jax.nn.one_hot(top_i, NUM_EXPERTS, dtype=x.dtype) * gates[..., None], axis=-2)
        out = jnp.zeros_like(x)
        for e in range(NUM_EXPERTS):
            h = jax.nn.relu(jnp.einsum('bsd,fd->bsf', x, w1[e]))
            y = jnp.einsum('bsf,df->bsd', h, w2[e])
            out = out + combine[..., e, None] * y
        return out

    def _L1_xattn_ref(query, key, value, Wq, bq, Wk, bk, Wv, bv, Wo, bo):
        import jax, jax.numpy as jnp
        import numpy as np
        B, S, D, H = (4, 256, 128, 16)
        HD = D // H
        b = query.shape[0]
        Q = (query @ Wq + bq).reshape(b, -1, H, HD).transpose(0, 2, 1, 3)
        K = (key @ Wk + bk).reshape(b, -1, H, HD).transpose(0, 2, 1, 3)
        V = (value @ Wv + bv).reshape(b, -1, H, HD).transpose(0, 2, 1, 3)
        energy = jnp.einsum('bhqd,bhkd->bhqk', Q, K) / np.sqrt(HD)
        attn = jax.nn.softmax(energy, axis=-1)
        x = jnp.einsum('bhqk,bhkd->bhqd', attn, V)
        x = x.transpose(0, 2, 1, 3).reshape(b, -1, H * HD)
        return x @ Wo + bo

    def _L1_ffn_ref(x, Wr, W1, b1, W2, b2):
        import jax, jax.numpy as jnp
        import numpy as np
        B, S, H, M, E, K = (4, 256, 128, 512, 8, 2)
        logits = jnp.einsum('bsh,eh->bse', x, Wr)
        probs = jax.nn.softmax(logits, axis=-1)
        top_v, top_i = jax.lax.top_k(probs, K)
        top_v = top_v / jnp.sum(top_v, axis=-1, keepdims=True)
        out = jnp.zeros_like(x)
        for e in range(E):
            w_e = jnp.sum(jnp.where(top_i == e, top_v, 0.0), axis=-1)
            h = jnp.einsum('bsh,mh->bsm', x, W1[e]) + b1[e]
            h = jax.nn.gelu(h, approximate=False)
            y = jnp.einsum('bsm,hm->bsh', h, W2[e]) + b2[e]
            out = out + y * w_e[..., None]
        return out

    def _L2_xattn_ref(input_tensor, encoder_output, Wq1, Wk1, Wv1, bv1, Wq2, Wk2, Wv2, bv2, g1, be1, g2, be2, g3, be3, Wf1, bf1, Wf2, bf2):
        import jax, jax.numpy as jnp
        import numpy as np
        D_MODEL = 128
        N_HEADS = 16
        HEAD = D_MODEL // N_HEADS
        D_FF = 512
        LN_EPS = 1e-05

        def _layernorm(x, g, b):
            mu = jnp.mean(x, axis=-1, keepdims=True)
            var = jnp.mean(jnp.square(x - mu), axis=-1, keepdims=True)
            return (x - mu) * jax.lax.rsqrt(var + LN_EPS) * g + b

        def _mha(q_in, k_in, v_in, Wq, Wk, Wv, bv, causal):
            q = jnp.einsum('bsd,hde->bhse', q_in, Wq)
            k = jnp.einsum('btd,hde->bhte', k_in, Wk)
            v = jnp.einsum('btd,hde->bhte', v_in, Wv) + bv[None, :, None, :]
            scale = HEAD ** (-0.5)
            scores = jnp.einsum('bhse,bhte->bhst', q, k) * scale
            if causal:
                S, T = (scores.shape[-2], scores.shape[-1])
                mask = jnp.tril(jnp.ones((S, T), dtype=bool))
                scores = jnp.where(mask, scores, -jnp.inf)
            p = jax.nn.softmax(scores, axis=-1)
            o = jnp.einsum('bhst,bhte->bhse', p, v)
            B, H, S, E = o.shape
            return o.transpose(0, 2, 1, 3).reshape(B, S, H * E)
        x = input_tensor
        sa = _mha(x, x, x, Wq1, Wk1, Wv1, bv1, causal=True)
        x = _layernorm(sa + input_tensor, g1, be1)
        ca = _mha(x, encoder_output, encoder_output, Wq2, Wk2, Wv2, bv2, causal=False)
        x = _layernorm(x + ca, g2, be2)
        ffn = jax.nn.relu(x @ Wf1 + bf1) @ Wf2 + bf2
        x = _layernorm(x + ffn, g3, be3)
        return x

    def _L2_ffn_ref(x, rW1, rb1, ln_g, ln_b, rW2, rb2, qW, qb, kW, kb, vW, vb, oW, ob):
        import jax, jax.numpy as jnp
        import numpy as np
        H = 16
        TOP_K = 2
        LN_EPS = 1e-05
        B, S, E = x.shape
        NE = qW.shape[0]
        Dh = E // H
        scale = 1.0 / jnp.sqrt(jnp.asarray(Dh, x.dtype))
        h = x @ rW1.T + rb1
        mu = h.mean(-1, keepdims=True)
        var = ((h - mu) ** 2).mean(-1, keepdims=True)
        h = (h - mu) * jax.lax.rsqrt(var + LN_EPS) * ln_g + ln_b
        h = jax.nn.relu(h)
        logits = h @ rW2.T + rb2
        probs = jax.nn.softmax(logits, axis=-1)
        tp, ti = jax.lax.top_k(probs, TOP_K)
        tp = tp / tp.sum(-1, keepdims=True)
        expert_mask = (jax.nn.one_hot(ti, NE, dtype=probs.dtype) * tp[..., None]).sum(-2)
        gates = jnp.moveaxis(expert_mask, -1, 0)

        def expert_step(acc, params):
            qw, qb_, kw, kb_, vw, vb_, ow, ob_, g = params
            q = (x @ qw.T + qb_).reshape(B, S, H, Dh).transpose(0, 2, 1, 3)
            k = (x @ kw.T + kb_).reshape(B, S, H, Dh).transpose(0, 2, 1, 3)
            v = (x @ vw.T + vb_).reshape(B, S, H, Dh).transpose(0, 2, 1, 3)
            scores = jnp.einsum('bhqd,bhkd->bhqk', q, k) * scale
            p = jax.nn.softmax(scores, axis=-1)
            o = jnp.einsum('bhqk,bhkd->bhqd', p, v)
            o = o.transpose(0, 2, 1, 3).reshape(B, S, E) @ ow.T + ob_
            return (acc + o * g[..., None], None)
        out, _ = jax.lax.scan(expert_step, jnp.zeros_like(x), (qW, qb, kW, kb, vW, vb, oW, ob, gates))
        return out

    def _L3_xattn_ref(query, key, value, q_w, q_b, k_w, k_b, v_w, v_b, o_w, o_b):
        import jax, jax.numpy as jnp
        import numpy as np
        EMBED_DIM = 128
        NUM_HEADS = 16
        HEAD_DIM = EMBED_DIM // NUM_HEADS
        WINDOW = 64

        def apply_rope(x):
            B, H, S, d = x.shape
            half = d // 2
            pos = jnp.arange(S, dtype=x.dtype)
            freqs = 1.0 / 10000.0 ** (jnp.arange(half, dtype=x.dtype) / half)
            ang = pos[:, None] * freqs[None, :]
            cos, sin = (jnp.cos(ang), jnp.sin(ang))
            x1, x2 = (x[..., :half], x[..., half:])
            return jnp.concatenate([x1 * cos - x2 * sin, x1 * sin + x2 * cos], axis=-1)

        def _forward(query, key, value, q_w, q_b, k_w, k_b, v_w, v_b, o_w, o_b):
            B, S_q, D = query.shape
            S_k = key.shape[1]
            H, d, W = (NUM_HEADS, HEAD_DIM, WINDOW)
            q = (query @ q_w.T + q_b).reshape(B, S_q, H, d).transpose(0, 2, 1, 3)
            k = (key @ k_w.T + k_b).reshape(B, S_k, H, d).transpose(0, 2, 1, 3)
            v = (value @ v_w.T + v_b).reshape(B, S_k, H, d).transpose(0, 2, 1, 3)
            q = apply_rope(q) * d ** (-0.5)
            k = apply_rope(k)
            q_pos = jnp.arange(S_q)[:, None]
            offsets = jnp.arange(-W, 1)[None, :]
            idx = q_pos + offsets
            local_mask = (idx < 0) | (idx >= S_k)
            gidx = jnp.clip(idx, 0, S_k - 1)
            k_win = k[:, :, gidx, :]
            v_win = v[:, :, gidx, :]
            scores = jnp.einsum('bhqd,bhqwd->bhqw', q, k_win)
            mask = local_mask[None, None, :, :]
            scores = jnp.where(mask, -jnp.inf, scores)
            m = jnp.max(scores, axis=-1, keepdims=True)
            m = jnp.where(jnp.isfinite(m), m, 0.0)
            e = jnp.exp(scores - m)
            denom = jnp.sum(e, axis=-1, keepdims=True)
            probs = jnp.where(denom > 0, e / jnp.where(denom > 0, denom, 1.0), 0.0)
            ctx = jnp.einsum('bhqw,bhqwd->bhqd', probs, v_win)
            ctx = ctx.transpose(0, 2, 1, 3).reshape(B, S_q, D)
            return ctx @ o_w.T + o_b
        return _forward(query, key, value, q_w, q_b, k_w, k_b, v_w, v_b, o_w, o_b)

    def _L3_ffn_ref(x, router_kernel_DE, kernel_gating_EDF, kernel_up_EDF, kernel_down_EFD):
        import jax, jax.numpy as jnp
        import numpy as np
        TOP_K = 2
        E = router_kernel_DE.shape[-1]
        x = x.astype(jnp.float32)
        logits_BSE = jnp.einsum('BSD,DE->BSE', x, router_kernel_DE)
        probs_BSE = jax.nn.softmax(logits_BSE.astype(jnp.float32), axis=-1)
        weights_BSK, indices_BSK = jax.lax.top_k(probs_BSE, TOP_K)
        norm_weights_BSK = jax.nn.softmax(weights_BSK, axis=-1)
        one_hot_BSKE = jax.nn.one_hot(indices_BSK, num_classes=E, dtype=x.dtype)
        full_weights_BSE = jnp.sum(one_hot_BSKE * norm_weights_BSK[..., None], axis=2)
        gating_BSEF = jnp.einsum('BSD,EDF->BSEF', x, kernel_gating_EDF)
        act_BSEF = jax.nn.silu(gating_BSEF)
        up_BSEF = jnp.einsum('BSD,EDF->BSEF', x, kernel_up_EDF)
        fuse_BSEF = act_BSEF * up_BSEF
        down_BSED = jnp.einsum('BSEF,EFD->BSED', fuse_BSEF, kernel_down_EFD)
        out_BSD = jnp.einsum('BSED,BSE->BSD', down_BSED, full_weights_BSE)
        return out_BSD.astype(jnp.float32)
    x = x + _L0_xattn_ref(_layernorm(x, axis=-1), ctx_1024, ctx_1024, L0_xattn_Wq, L0_xattn_Wk, L0_xattn_Wv, L0_xattn_Wo, L0_xattn_bq, L0_xattn_bk, L0_xattn_bv, L0_xattn_bo)
    x = x + _L0_ffn_ref(_layernorm(x, axis=-1), L0_ffn_gate_w, L0_ffn_w1, L0_ffn_w2)
    x = x + _L1_xattn_ref(_layernorm(x, axis=-1), ctx_1024, ctx_1024, L1_xattn_Wq, L1_xattn_bq, L1_xattn_Wk, L1_xattn_bk, L1_xattn_Wv, L1_xattn_bv, L1_xattn_Wo, L1_xattn_bo)
    x = x + _L1_ffn_ref(_layernorm(x, axis=-1), L1_ffn_Wr, L1_ffn_W1, L1_ffn_b1, L1_ffn_W2, L1_ffn_b2)
    x = x + _L2_xattn_ref(_layernorm(x, axis=-1), ctx_1024, L2_xattn_Wq1, L2_xattn_Wk1, L2_xattn_Wv1, L2_xattn_bv1, L2_xattn_Wq2, L2_xattn_Wk2, L2_xattn_Wv2, L2_xattn_bv2, L2_xattn_g1, L2_xattn_be1, L2_xattn_g2, L2_xattn_be2, L2_xattn_g3, L2_xattn_be3, L2_xattn_Wf1, L2_xattn_bf1, L2_xattn_Wf2, L2_xattn_bf2)
    x = x + _L2_ffn_ref(_layernorm(x, axis=-1), L2_ffn_rW1, L2_ffn_rb1, L2_ffn_ln_g, L2_ffn_ln_b, L2_ffn_rW2, L2_ffn_rb2, L2_ffn_qW, L2_ffn_qb, L2_ffn_kW, L2_ffn_kb, L2_ffn_vW, L2_ffn_vb, L2_ffn_oW, L2_ffn_ob)
    x = x + _L3_xattn_ref(_layernorm(x, axis=-1), ctx_1024, ctx_1024, L3_xattn_q_w, L3_xattn_q_b, L3_xattn_k_w, L3_xattn_k_b, L3_xattn_v_w, L3_xattn_v_b, L3_xattn_o_w, L3_xattn_o_b)
    x = x + _L3_ffn_ref(_layernorm(x, axis=-1), L3_ffn_router_kernel_DE, L3_ffn_kernel_gating_EDF, L3_ffn_kernel_up_EDF, L3_ffn_kernel_down_EFD)
    return x

_drawn_inputs = setup_inputs


def setup_inputs(seed=0):
    import zlib

    import numpy as np

    out = dict(_drawn_inputs(seed))
    spreads = {'L0_xattn_bq': (0.0, 0.348),
     'L0_xattn_bk': (0.0, 0.8),
     'L0_xattn_bv': (0.0, 0.1),
     'L0_xattn_bo': (0.0, 0.1),
     'L1_xattn_bq': (0.0, 0.1),
     'L1_xattn_bk': (0.0, 0.8),
     'L1_xattn_bv': (0.0, 0.1),
     'L1_xattn_bo': (0.0, 0.1),
     'L2_xattn_bv1': (0.0, 0.1),
     'L2_xattn_bv2': (0.0, 0.1),
     'L2_xattn_g1': (1.0, 0.2),
     'L2_xattn_be1': (0.0, 0.1),
     'L2_xattn_g2': (1.0, 0.2),
     'L2_xattn_be2': (0.0, 0.1),
     'L2_xattn_g3': (1.0, 0.2),
     'L2_xattn_be3': (0.0, 0.1),
     'L2_xattn_bf1': (0.0, 0.28),
     'L2_xattn_bf2': (0.0, 0.1),
     'L2_ffn_rb1': (0.0, 0.343),
     'L2_ffn_ln_g': (1.0, 0.6),
     'L2_ffn_ln_b': (0.0, 0.8),
     'L2_ffn_rb2': (0.0, 0.1),
     'L2_ffn_qb': (0.0, 0.8),
     'L2_ffn_kb': (0.0, 0.8),
     'L2_ffn_vb': (0.0, 0.8),
     'L2_ffn_ob': (0.0, 0.1)}
    factors = {'L1_ffn_b1': 8.0,
     'L1_ffn_b2': 8.0,
     'L2_ffn_qW': 8.0,
     'L2_ffn_kW': 8.0,
     'L2_ffn_vW': 5.781,
     'L2_ffn_oW': 4.377,
     'L3_xattn_q_b': 8.0,
     'L3_xattn_k_b': 8.0,
     'L3_xattn_v_b': 8.0,
     'L3_xattn_o_b': 8.0,
     'L3_ffn_router_kernel_DE': 8.0,
     'L3_ffn_kernel_gating_EDF': 8.0,
     'L3_ffn_kernel_up_EDF': 8.0,
     'L3_ffn_kernel_down_EFD': 8.0}
    for name, (base, spread) in spreads.items():
        noise = np.random.default_rng([zlib.crc32(name.encode()), seed]).standard_normal(out[name].shape)
        drawn = base * np.exp(spread * noise) if base else spread * noise
        out[name] = jnp.asarray(drawn.astype(out[name].dtype))
    for name, factor in factors.items():
        out[name] = (out[name] * factor).astype(out[name].dtype)
    return out
```

```python
from contextlib import ExitStack

import numpy as np

import concourse.bass as bass
from concourse import mybir

F32 = mybir.dt.float32
BF16 = mybir.dt.bfloat16
ALU = mybir.AluOpType
ACT = mybir.ActivationFunctionType
AX = mybir.AxisListType

P = 128
NSEQ = 32
NB = 4
GROUPS = NSEQ // NB
NT = NB * P
H = 16
D = P // H
BANDS = 4
HB = H // BANDS
NE = 8
SCALE = float(D) ** -0.5
EPS = 1e-5
WINDOW = 64
NORMS = 12
NEG = -1e30
CONSTS = 6
CH = 4
CH3 = 2


class Tally:

    def __init__(self, totals, base):
        self.totals, self.base, self.n = totals, base, {}

    def next(self, name, k=1):
        self.n[name] = self.n.get(name, 0) + k
        return self.at(name, self.n[name])

    def at(self, name, n):
        return self.base * self.totals.get(name, 0) + n


class Ring:

    def __init__(self, tally, name, banks):
        self.tally, self.name, self.banks, self.used = tally, name, banks, []
        self.count = {"act": 0, "dve": 0}

    def fill(self, consumer):
        n = len(self.used)
        self.count[consumer] += 1
        self.used.append((consumer, self.count[consumer]))
        old = self.taken(n - len(self.banks)) if n >= len(self.banks) else None
        return self.banks[n % len(self.banks)], self.tally.at(f"{self.name}_filled", n + 1), self.taken(n), old

    def taken(self, n):
        who, count = self.used[n]
        name = f"{self.name}_taken_{who}"
        return name, self.tally.at(name, count)


RINGS = {"s1": (0, 1), "s2": (2, 3), "o": (4, 5), "g": (6, 7)}
SIGNALS = [f"{r}_{s}" for r in RINGS for s in ("filled", "taken_act", "taken_dve")] + [
    "ln_ready",
    "split_ready",
    "weighed",
    "r_ready",
    "router_in",
    "router_exp",
    "wts_ready",
    "var_ready",
    "rstd_ready",
    "out_ready",
    "dve_step"]

PROJ = ["L0q", "L0k", "L0v", "L0o", "L1q", "L1k", "L1v", "L1o", "L2q1", "L2k1", "L2v1", "L2q2", "L2k2",
        "L2v2", "L3q", "L3qs", "L3k", "L3ks", "L3v", "L3o"] + [f"E{m}{e}" for e in range(NE) for m in "qkvo"]
COLS = ["L0q", "L0k", "L1q", "L1k", "L3q", "L3qs", "L3k", "L3ks"] + [f"E{m}{e}" for e in range(NE) for m in "qk"] \
    + [f"f1{c}" for c in range(CH)] + [f"b1{e}{c}" for e in range(NE) for c in range(CH)]
ROWS = ["L0v", "L0o", "L1v", "L1o", "L2v1", "L2v2", "L3v", "L3o", "g1", "be1", "g2", "be2", "g3", "be3",
        "bf2"] + [f"Ev{e}" for e in range(NE)]


def build(nc, A, out, totals):
    with ExitStack() as ctx:
        def sb(name, shape, dt=F32):
            return ctx.enter_context(nc.sbuf_tensor(name, shape, dt))

        sem = {n: ctx.enter_context(nc.semaphore(n)) for n in SIGNALS}
        weights_in = ctx.enter_context(nc.semaphore("weights_in"))
        x_in = ctx.enter_context(nc.semaphore("x_in"))
        staged_used = ctx.enter_context(nc.semaphore("staged_used"))
        stored = ctx.enter_context(nc.semaphore("stored"))
        consts_set = ctx.enter_context(nc.semaphore("consts_set"))
        bank = [ctx.enter_context(nc.psum_tensor(f"bank{i}", [P, 512], F32)) for i in range(8)]

        wproj = sb("wproj", [P, len(PROJ), P])
        wf = {n: sb(n, [P, s]) for n, s in (("w1_0", NE * 512), ("w2_0", NE * CH * P), ("w1_1", NE * 512),
                                           ("w2_1", NE * CH * P), ("gate_3", NE * 256), ("up_3", NE * 256),
                                           ("down_3", NE * CH3 * P), ("wf1", 512), ("wf2", CH * P))}
        router = sb("router", [P, 3, NE])
        rw1 = sb("rw1", [P, P // 2])
        rw2 = sb("rw2", [P // 2, NE])
        cols = sb("cols", [P, len(COLS)])
        rows = sb("rows", [P, len(ROWS), P])
        rrow = sb("rrow", [P, 3, P // 2])
        rb2 = sb("rb2", [P, NE])
        ebias = sb("ebias", [NE, 2, P])
        rope = sb("rope", [P, 2, P])
        ident = sb("ident", [P, P])
        identb = sb("identb", [P, 2, P], BF16)
        masks = sb("masks", [P, 4, P], BF16)
        band = sb("band", [P, HB])
        tri = sb("tri", [P, NE, NE])

        x_st = sb("x_st", [P, NB, P])
        c_st = sb("c_st", [P, NB, P])
        x_tok = sb("x_tok", [P, NB, P])
        out_tok = sb("out_tok", [P, NB, P])
        h_tok = sb("h_tok", [P, NB, P])
        hh_tok = sb("hh_tok", [P, NB, P])
        ctxT = sb("ctxT", [P, NT])
        hT = sb("hT", [P, NT])
        stats = sb("stats", [P, NB, 6])
        mv = sb("mv", [P, NB, 2])
        rstd = sb("rstd", [P, NB])
        power = sb("power", [P, NB])
        qf = sb("qf", [P, NT])
        kf = sb("kf", [P, NT])
        qs = sb("qs", [P, NT])
        ks = sb("ks", [P, NT])
        qb = sb("qb", [P, NT], BF16)
        qm = sb("qm", [P, HB, NT])
        km = sb("km", [P, HB, NT], BF16)
        vaug = sb("vaug", [P, NB, H, D + 1])
        mx = sb("mx", [P, NB, H], BF16)
        ex = sb("ex", [P, 2, HB, P])
        rden = sb("rden", [P, NB, H])
        att_tok = sb("att_tok", [P, NB, P])
        attT = sb("attT", [P, NT])
        hid = sb("hid", [P, 2, CH, NT])
        sg = sb("sg", [P, 2, NT])
        logit = sb("logit", [P, NB, NE])
        lmax = sb("lmax", [P, NB])
        cmp1 = sb("cmp1", [P, NB, NE, NE])
        cmp2 = sb("cmp2", [P, NB, NE, NE])
        top = sb("top", [P, NB, NE])
        lex = sb("lex", [P, NB, NE])
        wts = sb("wts", [P, NB, NE])
        wtsT = sb("wtsT", [NE, NT])
        lsum = sb("lsum", [P, NB])
        r_full = sg[:, 0, :].rearrange("p (b f) -> p b f", b=NB)
        r_tok = r_full[:, :, 0:P // 2]
        rT = qs[0:P // 2, :]

        loads = [(wproj, A["wproj"]), (router, A["router"]), (rw1, A["rw1"]), (rw2, A["rw2"]), (cols, A["cols"]),
                 (rope, A["rope"]), (ident, A["ident"]),
                 (band, A["band"]), (ebias, A["ebias"])] + [(wf[n], A[n]) for n in wf]
        spread = [(rows, A["rows"]), (rrow, A["rrow"]), (rb2, A["rb2"]), (tri, A["tri"])]
        masks_f32 = hid[:, 0, 0, :].rearrange("p (m k) -> p m k", m=4)
        n_loads = len(loads) + len(spread) + 1

        x_dram = A["x"].rearrange("(g b) t f -> g t b f", b=NB)
        c_dram = A["ctx"].rearrange("(g b) t f -> g t b f", b=NB)
        o_dram = out.rearrange("(g b) t f -> g t b f", b=NB)

        def W(name):
            return wproj[:, PROJ.index(name), :]

        def col(name):
            return cols[:, COLS.index(name):COLS.index(name) + 1]

        def over_seqs(ap):
            return ap.unsqueeze(1).to_broadcast([P, NB, ap.shape[1]])

        def row(name):
            return over_seqs(rows[:, ROWS.index(name), :])

        def b4(ap):
            return ap.rearrange("p (b t) -> p b t", b=NB)

        block = ctx.enter_context(nc.Block())
        counted = {}

        @block.sync
        def _(sp):
            for dst, src in loads:
                sp.dma_start(dst[:], src).then_inc(weights_in, 16)
            sp.dma_start(masks_f32, A["masks"]).then_inc(weights_in, 16)
            for dst, src in spread:
                sp.dma_start(dst[:], src.unsqueeze(0).to_broadcast(list(dst.shape))).then_inc(weights_in, 16)
            with sp.Fori(0, GROUPS) as g:
                sp.wait_ge(staged_used, g * 2)
                sp.dma_start(x_st[:], x_dram[g]).then_inc(x_in, 16)
                sp.dma_start(c_st[:], c_dram[g]).then_inc(x_in, 16)

        @block.gpsimd
        def _(pool):
            pool.memset(vaug[:], 1.0).then_inc(consts_set, 1)
            pool.memset(power[:], -0.5).then_inc(consts_set, 1)
            pool.memset(sg[:], 0.0).then_inc(consts_set, 1)
            pool.wait_ge(consts_set, CONSTS)
            with pool.Fori(0, GROUPS) as g:
                t = Tally(totals, g)
                for _ in range(NORMS):
                    pool.wait_ge(sem["var_ready"], t.next("var_ready"))
                    nc.gpsimd.tensor_tensor(rstd[:], rstd[:], power[:], ALU.pow).then_inc(sem["rstd_ready"], 1)
                pool.wait_ge(sem["out_ready"], g + 1)
                pool.dma_start(o_dram[g], out_tok[:]).then_inc(stored, 16)
            pool.wait_ge(stored, 16 * GROUPS)

        @block.tensor
        def _(pe):
            pe.wait_ge(weights_in, 16 * n_loads)
            pe.wait_ge(consts_set, CONSTS)
            with pe.Fori(0, GROUPS) as g:
                t = Tally(totals, g)
                ring = {n: Ring(t, n, b) for n, b in RINGS.items()}
                pe.wait_ge(sem["out_ready"], g)

                def open_bank(name, consumer):
                    b, _, taken, old = ring[name].fill(consumer)
                    if old:
                        pe.wait_ge(sem[old[0]], old[1])
                    return bank[b], taken

                def wait_taken(taken):
                    pe.wait_ge(sem[taken[0]], taken[1])

                def to_T(src, ready, rows_=P):
                    pe.wait_ge(sem[ready[0]], ready[1])
                    ps, taken = open_bank("g", "act")
                    for b in range(NB):
                        mm = nc.tensor.transpose(ps[0:rows_, b * P:(b + 1) * P], src[:, b, :], ident[:])
                    mm.then_inc(sem["g_filled"], 1)
                    wait_taken(taken)

                def project(w, src):
                    ps, taken = open_bank("g", "act")
                    nc.tensor.matmul(ps[:], w, src[:], start=True, stop=True).then_inc(sem["g_filled"], 1)
                    return taken

                def by_token(w, src, n, k=P):
                    ps, taken = open_bank("g", "dve")
                    for b in range(NB):
                        mm = nc.tensor.matmul(ps[:, b * n:(b + 1) * n], src[0:k, b * P:(b + 1) * P], w,
                                              start=True, stop=True)
                    mm.then_inc(sem["g_filled"], 1)
                    return taken

                def attention(q, k, v, srcT, kvT, mask, rot):
                    for name, src in [(q, srcT), (k, kvT)] + ([(q + "s", srcT), (k + "s", kvT)] if rot else []):
                        taken = project(W(name), src)
                    wait_taken(taken)
                    wait_taken(by_token(W(v), kvT, P))
                    pe.wait_ge(sem["split_ready"], t.next("split_ready"))
                    units = [(b, j) for b in range(NB) for j in range(BANDS)]
                    o_bank, max_taken, exp_taken = {}, {}, {}

                    def scores(b, j):
                        p, s = slice(32 * j, 32 * j + 32), slice(b * P, (b + 1) * P)
                        ps, max_taken[b, j] = open_bank("s1", "dve")
                        mm = nc.tensor.matmul(ps[:], qb[p, s], km[p, :, s], start=True, stop=mask is None)
                        if mask is not None:
                            mm = nc.tensor.matmul(ps[:], identb[:, 0, :], masks[:, 2 * mask, :].unsqueeze(1)
                                                  .to_broadcast([P, HB, P]), start=False, stop=True)
                        mm.then_inc(sem["s1_filled"], 1)

                    def scores_t(b, j):
                        p, s = slice(32 * j, 32 * j + 32), slice(b * P, (b + 1) * P)
                        ps, exp_taken[b, j] = open_bank("s2", "act")
                        nc.tensor.matmul(ps[:], kf[p, s], qm[p, :, s], start=True, stop=False)
                        if mask is not None:
                            nc.tensor.matmul(ps[:], identb[:, 0, :], masks[:, 2 * mask + 1, :].unsqueeze(1)
                                             .to_broadcast([P, HB, P]), start=False, stop=False)
                        wait_taken(max_taken[b, j])
                        for i in range(HB):
                            h = HB * j + i
                            mm = nc.tensor.matmul(ps[:, i * P:(i + 1) * P], mx[:, b, h:h + 1].to_broadcast([P, P]),
                                                  identb[:, 1, :], start=False, stop=i == HB - 1)
                        mm.then_inc(sem["s2_filled"], 1)

                    def weigh(n, b, j):
                        if j == 0:
                            o_bank[b] = open_bank("o", "dve")
                        wait_taken(exp_taken[b, j])
                        for i in range(HB):
                            h = HB * j + i
                            mm = nc.tensor.matmul(o_bank[b][0][:, h * (D + 1):(h + 1) * (D + 1)], ex[:, n % 2, i, :],
                                                  vaug[:, b, h, :], start=True, stop=True)
                        mm.then_inc(sem["weighed"], 1)

                    for n in range(len(units) + 2):
                        if n < len(units):
                            scores(*units[n])
                        if 1 <= n <= len(units):
                            scores_t(*units[n - 1])
                        if n >= 2:
                            weigh(n - 2, *units[n - 2])
                    return o_bank[NB - 1][1]

                def out_proj(w, attended):
                    to_T(att_tok, attended)
                    by_token(w, attT, P)

                def experts(w1, w2, chunks, kinds):
                    taken = {}

                    def first(e):
                        for c in range(chunks):
                            for w, who in zip(w1, kinds):
                                ps, taken[e] = open_bank("s1", who)
                                at = (e * chunks + c) * P
                                nc.tensor.matmul(ps[:], w[:, at:at + P], hT[:], start=True, stop=True)\
                                    .then_inc(sem["s1_filled"], 1)

                    def second(e):
                        wait_taken(taken[e])
                        ps, _ = open_bank("s2", "dve")
                        for b in range(NB):
                            for c in range(chunks):
                                at = (e * chunks + c) * P
                                mm = nc.tensor.matmul(ps[:, b * P:(b + 1) * P], hid[:, e % 2, c, b * P:(b + 1) * P],
                                                      w2[:, at:at + P], start=c == 0, stop=c == chunks - 1)
                        mm.then_inc(sem["s2_filled"], 1)
                    return first, second

                def mixture(w1, w2, chunks, kinds):
                    first, second = experts(w1, w2, chunks, kinds)
                    for e in range(NE + 1):
                        if e < NE:
                            first(e)
                        if e:
                            second(e - 1)

                def expert_biases(k):
                    to_T(wts, ("wts_ready", t.next("wts_ready")), NE)
                    by_token(ebias[:, k, :], wtsT, P, NE)

                def to_hT():
                    to_T(h_tok, ("ln_ready", t.next("ln_ready")))

                pe.wait_ge(x_in, g * 32 + 32)
                ps, taken = open_bank("g", "act")
                for b in range(NB):
                    mm = nc.tensor.transpose(ps[:, b * P:(b + 1) * P], c_st[:, b, :], ident[:])
                mm.then_inc(sem["g_filled"], 1)
                wait_taken(taken)
                pe.sem_inc(staged_used, 1)
                to_hT()
                out_proj(W("L0o"), attention("L0q", "L0k", "L0v", hT, ctxT, 0, False))
                to_hT()
                by_token(router[:, 0, :], hT, NE)
                mixture([wf["w1_0"]], wf["w2_0"], CH, ["act"])
                to_hT()
                out_proj(W("L1o"), attention("L1q", "L1k", "L1v", hT, ctxT, None, False))
                to_hT()
                by_token(router[:, 1, :], hT, NE)
                expert_biases(0)
                mixture([wf["w1_1"]], wf["w2_1"], CH, ["act"])
                to_hT()
                attention("L2q1", "L2k1", "L2v1", hT, hT, 0, False)
                to_hT()
                attention("L2q2", "L2k2", "L2v2", hT, ctxT, None, False)
                to_hT()
                first, second = experts([wf["wf1"]], wf["wf2"], CH, ["act"])
                first(0)
                second(0)
                to_hT()
                by_token(rw1[:], hT, P // 2)
                to_T(r_full, ("r_ready", t.next("r_ready")))
                by_token(rw2[:], rT, NE, P // 2)
                expert_biases(1)
                for e in range(NE):
                    out_proj(W(f"Eo{e}"), attention(f"Eq{e}", f"Ek{e}", f"Ev{e}", hT, hT, None, False))
                to_hT()
                out_proj(W("L3o"), attention("L3q", "L3k", "L3v", hT, ctxT, 1, True))
                to_hT()
                by_token(router[:, 2, :], hT, NE)
                mixture([wf["gate_3"], wf["up_3"]], wf["down_3"], CH3, ["act", "dve"])
            counted["pe"] = (t, ring)

        @block.scalar
        def _(act):
            act.wait_ge(weights_in, 16 * n_loads)
            act.wait_ge(consts_set, CONSTS)
            with act.Fori(0, GROUPS) as g:
                t = Tally(totals, g)
                ring = {n: Ring(t, n, b) for n, b in RINGS.items()}

                def take(name):
                    b, full, _, _ = ring[name].fill("act")
                    act.wait_ge(sem[name + "_filled"], full)
                    return bank[b]

                def skip(name, n=1):
                    for _ in range(n):
                        ring[name].fill("dve")

                def evacuate(dst, parts=P):
                    ps = take("g")
                    nc.scalar.activation(dst, ps[0:parts, :], ACT.Copy).then_inc(sem["g_taken_act"], 1)

                def attention(bias, rot, q, k):
                    for dst, name in [(qf, q), (kf, k)] + ([(qs, q + "s"), (ks, k + "s")] if rot else []):
                        ps = take("g")
                        if bias:
                            ins = nc.scalar.activation(dst[:], ps[:], ACT.Identity, bias=col(name))
                        else:
                            ins = nc.scalar.activation(dst[:], ps[:], ACT.Copy)
                        ins.then_inc(sem["g_taken_act"], 1)
                    skip("g")
                    for n in range(NB * BANDS):
                        skip("s1")
                        ps = take("s2")
                        before = t.n.get("weighed", 0)
                        if before >= 2:
                            act.wait_ge(sem["weighed"], t.at("weighed", before - 1))
                        t.next("weighed")
                        ins = nc.scalar.activation(ex[:, n % 2, :, :], ps[:].rearrange("p (i q) -> p i q", i=HB),
                                                   ACT.Exp, scale=SCALE)
                        ins.then_inc(sem["s2_taken_act"], 1)

                def out_proj():
                    evacuate(attT[:])
                    skip("g")

                def gates(times=1):
                    skip("g")
                    for _ in range(times):
                        act.wait_ge(sem["router_in"], t.next("router_in"))
                        nc.scalar.activation(lex[:], logit[:], ACT.Exp)\
                            .then_inc(sem["router_exp"], 1)

                def mixture(func, ne, biases=None):
                    for e in range(ne):
                        for c in range(CH):
                            ps = take("s1")
                            kw = {"bias": col(biases(e, c))} if biases else {}
                            ins = nc.scalar.activation(hid[:, e % 2, c, :], ps[:], func, **kw)
                            ins.then_inc(sem["s1_taken_act"], 1)
                        skip("s2")

                def expert_biases():
                    evacuate(wtsT[:], NE)
                    skip("g")

                evacuate(ctxT[:])
                evacuate(hT[:])
                attention(True, False, "L0q", "L0k")
                out_proj()
                evacuate(hT[:])
                gates()
                mixture(ACT.Relu, NE)
                evacuate(hT[:])
                attention(True, False, "L1q", "L1k")
                out_proj()
                evacuate(hT[:])
                gates()
                expert_biases()
                mixture(ACT.Gelu, NE, lambda e, c: f"b1{e}{c}")
                evacuate(hT[:])
                attention(False, False, "L2q1", "L2k1")
                evacuate(hT[:])
                attention(False, False, "L2q2", "L2k2")
                evacuate(hT[:])
                mixture(ACT.Relu, 1, lambda e, c: f"f1{c}")
                evacuate(hT[:])
                skip("g")
                evacuate(rT[:], P // 2)
                gates()
                expert_biases()
                for e in range(NE):
                    attention(True, False, f"Eq{e}", f"Ek{e}")
                    out_proj()
                evacuate(hT[:])
                attention(True, True, "L3q", "L3k")
                out_proj()
                evacuate(hT[:])
                gates(2)
                multiplied = []
                for e in range(NE):
                    for c in range(CH3):
                        ps = take("s1")
                        multiplied.append(ring["s1"].fill("dve")[2])
                        n = e * CH3 + c
                        if n >= 2:
                            act.wait_ge(sem[multiplied[n - 2][0]], multiplied[n - 2][1])
                        nc.scalar.activation(sg[:, n % 2, :], ps[:], ACT.Silu).then_inc(sem["s1_taken_act"], 1)
                    skip("s2")
            counted["act"] = (t, ring)

        @block.vector
        def _(dve):
            dve.wait_ge(weights_in, 16 * n_loads)
            nc.vector.tensor_copy(masks[:], masks_f32).then_inc(consts_set, 1)
            nc.vector.tensor_copy(identb[:, 0, :], ident[:]).then_inc(consts_set, 1)
            nc.vector.tensor_scalar(identb[:, 1, :], ident[:], -1.0, None, ALU.mult).then_inc(consts_set, 1)
            dve.wait_ge(consts_set, CONSTS)
            with dve.Fori(0, GROUPS) as g:
                t = Tally(totals, g)
                ring = {n: Ring(t, n, b) for n, b in RINGS.items()}

                def settle(ins, name="dve_step"):
                    ins.then_inc(sem[name], 1)
                    dve.wait_ge(sem[name], t.next(name))

                def settle_taken(ins, taken):
                    ins.then_inc(sem[taken[0]], 1)
                    dve.wait_ge(sem[taken[0]], taken[1])

                def take(name):
                    b, full, taken, _ = ring[name].fill("dve")
                    dve.wait_ge(sem[name + "_filled"], full)
                    return bank[b], taken

                def skip(name, n=1):
                    for _ in range(n):
                        taken = ring[name].fill("act")[2]
                    return taken

                def normalize(src, dst, n=P, gain=None, shift=None, relu=False):
                    for b in range(NB):
                        ins = nc.vector.bn_stats(stats[:, b, :], src[:, b, :])
                    settle(ins)
                    nc.vector.memset(rstd[:], 0.0)
                    for b in range(NB):
                        ins = nc.vector.bn_aggr(mv[:, b, :], stats[:, b, :])
                    settle(ins)
                    nc.vector.tensor_scalar(rstd[:], mv[:, :, 1], EPS, None, ALU.add)\
                        .then_inc(sem["var_ready"], 1)
                    t.next("var_ready")
                    dve.wait_ge(sem["rstd_ready"], t.next("rstd_ready"))
                    for b in range(NB):
                        ins = nc.vector.tensor_scalar(dst[:, b, :], src[:, b, :], mv[:, b, 0:1], rstd[:, b:b + 1],
                                                      ALU.subtract, ALU.mult)
                    if gain is not None:
                        settle(ins)
                        settle(nc.vector.tensor_tensor(dst[:], dst[:], gain, ALU.mult))
                        ins = nc.vector.tensor_tensor(dst[:], dst[:], shift, ALU.add)
                        if relu:
                            settle(ins)
                            ins = nc.vector.tensor_scalar(dst[:], dst[:], 0.0, None, ALU.max)
                    return ins

                def norm_to_hT(src, **kw):
                    settle(normalize(src, h_tok, **kw), "ln_ready")
                    skip("g")

                def attention(v, mask, rot):
                    projected = skip("g", 4 if rot else 2)
                    ps, taken = take("g")
                    for b in range(NB):
                        ins = nc.vector.tensor_tensor(vaug[:, b, :, 0:D],
                                                      ps[:, b * P:(b + 1) * P].rearrange("p (h d) -> p h d", d=D),
                                                      rows[:, ROWS.index(v), :].rearrange("p (h d) -> p h d", d=D),
                                                      ALU.add)
                    ins.then_inc(sem[taken[0]], 1)
                    dve.wait_ge(sem[projected[0]], projected[1])
                    if rot:
                        for a, s in ((qf, qs), (kf, ks)):
                            nc.vector.tensor_tensor(b4(a[:]), b4(a[:]), over_seqs(rope[:, 0, :]), ALU.mult)
                            settle(nc.vector.tensor_tensor(b4(s[:]), b4(s[:]), over_seqs(rope[:, 1, :]), ALU.mult))
                            settle(nc.vector.tensor_tensor(a[:], a[:], s[:], ALU.add))
                    nc.vector.tensor_copy(qb[:], qf[:])
                    for i in range(HB):
                        nc.vector.tensor_scalar(km[:, i, :], kf[:], band[:, i:i + 1], None, ALU.mult)
                    for i in range(HB):
                        ins = nc.vector.tensor_scalar(qm[:, i, :], qf[:], band[:, i:i + 1], None, ALU.mult)
                    ins.then_inc(sem["split_ready"], 1)

                    def maximum(b, j):
                        ps, taken = take("s1")
                        ins = nc.vector.tensor_reduce(mx[:, b, HB * j:HB * j + HB],
                                                      ps[:].rearrange("p (i k) -> p i k", i=HB), AX.X, ALU.max)
                        ins.then_inc(sem[taken[0]], 1)
                        skip("s2")

                    def divide(b):
                        b_, _, taken, _ = ring["o"].fill("dve")
                        dve.wait_ge(sem["weighed"], t.next("weighed", BANDS))
                        ps = bank[b_][:, 0:H * (D + 1)].rearrange("p (h d) -> p h d", d=D + 1)
                        settle(nc.vector.reciprocal(rden[:, b, :], ps[:, :, D]))
                        ins = nc.vector.tensor_tensor(att_tok[:, b, :].rearrange("p (h d) -> p h d", d=D),
                                                      ps[:, :, 0:D],
                                                      rden[:, b, :].unsqueeze(2).to_broadcast([P, H, D]), ALU.mult)
                        ins.then_inc(sem[taken[0]], 1)
                        return taken

                    for b in range(NB):
                        for j in range(BANDS):
                            maximum(b, j)
                            if b and j == 2:
                                divide(b - 1)
                    taken = divide(NB - 1)
                    dve.wait_ge(sem[taken[0]], taken[1])

                def out_proj():
                    skip("g")
                    return take("g")

                def residual(bias):
                    ps, taken = out_proj()
                    settle_taken(nc.vector.tensor_tensor(x_tok[:], x_tok[:], b4(ps[:]), ALU.add), taken)
                    settle(nc.vector.tensor_tensor(x_tok[:], x_tok[:], row(bias), ALU.add))

                def gates(bias=False, twice=False):
                    ps, taken = take("g")
                    lg = ps[:, 0:NB * NE].rearrange("p (b e) -> p b e", b=NB)
                    if bias:
                        ins = nc.vector.tensor_tensor(logit[:], lg, over_seqs(rb2[:]), ALU.add)
                    else:
                        ins = nc.vector.tensor_copy(logit[:], lg)
                    settle_taken(ins, taken)
                    nc.vector.tensor_reduce(lmax[:], logit[:], AX.X, ALU.max)
                    for b in range(NB):
                        other = logit[:, b, :].unsqueeze(1).to_broadcast([P, NE, NE])
                        own = logit[:, b, :].unsqueeze(2).to_broadcast([P, NE, NE])
                        nc.vector.tensor_tensor(cmp1[:, b], other, own, ALU.is_gt)
                        ins = nc.vector.tensor_tensor(cmp2[:, b], other, own, ALU.is_equal)
                    settle(ins)
                    settle(nc.vector.tensor_tensor(cmp2[:], cmp2[:], tri[:].unsqueeze(1)
                                                   .to_broadcast([P, NB, NE, NE]), ALU.mult))
                    settle(nc.vector.tensor_tensor(cmp1[:], cmp1[:], cmp2[:], ALU.add))
                    settle(nc.vector.tensor_reduce(top[:], cmp1[:], AX.X, ALU.add))
                    nc.vector.tensor_scalar(top[:], top[:], 1.5, None, ALU.is_lt)
                    ins = nc.vector.tensor_tensor(logit[:], logit[:], lmax[:].unsqueeze(2).to_broadcast([P, NB, NE]),
                                                  ALU.subtract)
                    ins.then_inc(sem["router_in"], 1)
                    t.next("router_in")

                    def exped():
                        dve.wait_ge(sem["router_exp"], t.next("router_exp"))

                    def share(dst):
                        settle(nc.vector.tensor_reduce(lsum[:], dst[:], AX.X, ALU.add))
                        settle(nc.vector.reciprocal(lsum[:], lsum[:]))
                        return nc.vector.tensor_tensor(dst[:], dst[:], lsum[:].unsqueeze(2)
                                                       .to_broadcast([P, NB, NE]), ALU.mult)
                    exped()
                    if twice:
                        settle(share(lex))
                        ins = nc.vector.tensor_tensor(logit[:], lex[:], lsum[:].unsqueeze(2)
                                                      .to_broadcast([P, NB, NE]), ALU.subtract)
                        ins.then_inc(sem["router_in"], 1)
                        t.next("router_in")
                        exped()
                    settle(nc.vector.tensor_tensor(wts[:], lex[:], top[:], ALU.mult))
                    return share(wts)

                def add_weighted(took, e):
                    ps, taken = took
                    for b in range(NB):
                        ins = nc.vector.scalar_tensor_tensor(x_tok[:, b, :], ps[:, b * P:(b + 1) * P],
                                                             wts[:, b, e:e + 1], x_tok[:, b, :], ALU.mult, ALU.add)
                    settle_taken(ins, taken)

                def expert_biases():
                    skip("g")
                    ps, taken = take("g")
                    settle_taken(nc.vector.tensor_tensor(x_tok[:], x_tok[:], b4(ps[:]), ALU.add), taken)

                def mixture():
                    for e in range(NE):
                        skip("s1", CH)
                        add_weighted(take("s2"), e)

                dve.wait_ge(x_in, g * 32 + 32)
                nc.vector.tensor_copy(x_tok[:], x_st[:]).then_inc(staged_used, 1)
                dve.wait_ge(staged_used, g * 2 + 2)
                skip("g")
                norm_to_hT(x_tok)
                attention("L0v", 0, False)
                residual("L0o")
                norm_to_hT(x_tok)
                settle(gates())
                mixture()
                norm_to_hT(x_tok)
                attention("L1v", None, False)
                residual("L1o")
                norm_to_hT(x_tok)
                settle(gates(), "wts_ready")
                expert_biases()
                mixture()
                norm_to_hT(x_tok)
                attention("L2v1", 0, False)
                settle(nc.vector.tensor_tensor(hh_tok[:], h_tok[:], att_tok[:], ALU.add))
                norm_to_hT(hh_tok, gain=row("g1"), shift=row("be1"))
                attention("L2v2", None, False)
                settle(nc.vector.tensor_tensor(hh_tok[:], h_tok[:], att_tok[:], ALU.add))
                norm_to_hT(hh_tok, gain=row("g2"), shift=row("be2"))
                skip("s1", CH)
                ps, taken = take("s2")
                settle_taken(nc.vector.tensor_tensor(hh_tok[:], h_tok[:], b4(ps[:]), ALU.add), taken)
                settle(nc.vector.tensor_tensor(hh_tok[:], hh_tok[:], row("bf2"), ALU.add))
                settle(normalize(hh_tok, h_tok, gain=row("g3"), shift=row("be3")))
                settle(nc.vector.tensor_tensor(x_tok[:], x_tok[:], h_tok[:], ALU.add))
                norm_to_hT(x_tok)
                ps, taken = take("g")
                ins = nc.vector.tensor_tensor(r_tok, ps[:, 0:NB * P // 2].rearrange("p (b f) -> p b f", b=NB),
                                              over_seqs(rrow[:, 0, :]), ALU.add)
                settle_taken(ins, taken)
                normalize(r_tok, r_tok, gain=over_seqs(rrow[:, 1, :]), shift=over_seqs(rrow[:, 2, :]), relu=True)\
                    .then_inc(sem["r_ready"], 1)
                t.next("r_ready")
                skip("g")
                settle(gates(bias=True), "wts_ready")
                expert_biases()
                for e in range(NE):
                    attention(f"Ev{e}", None, False)
                    add_weighted(out_proj(), e)
                norm_to_hT(x_tok)
                attention("L3v", 1, True)
                residual("L3o")
                norm_to_hT(x_tok)
                settle(gates(twice=True))

                def gate_hidden(e):
                    for c in range(CH3):
                        n = e * CH3 + c
                        silu = skip("s1")
                        dve.wait_ge(sem[silu[0]], silu[1])
                        ps, taken = take("s1")
                        ins = nc.vector.tensor_tensor(hid[:, e % 2, c, :], ps[:], sg[:, n % 2, :], ALU.mult)
                        ins.then_inc(sem[taken[0]], 1)

                for e in range(NE + 1):
                    if e < NE:
                        gate_hidden(e)
                    if e:
                        add_weighted(take("s2"), e - 1)
                dve.wait_ge(stored, g * 16)
                nc.vector.tensor_copy(out_tok[:], x_tok[:]).then_inc(sem["out_ready"], 1)
                dve.wait_ge(sem["out_ready"], t.next("out_ready"))
            counted["dve"] = (t, ring)
    return counted


def totals_of(counted):
    got = {}
    for t, ring in counted.values():
        for name, n in t.n.items():
            got[name] = max(got.get(name, 0), n)
        for r in ring.values():
            assert r.name == "o" or got.get(f"{r.name}_filled", len(r.used)) == len(r.used), r.name
            got[f"{r.name}_filled"] = max(len(r.used), got.get(f"{r.name}_filled", 0))
            for who, n in r.count.items():
                got[f"{r.name}_taken_{who}"] = max(n, got.get(f"{r.name}_taken_{who}", 0))
    return got


def laid_out(i):
    f = {k: np.asarray(v) for k, v in i.items()}

    def heads(w):
        return w.transpose(1, 0, 2).reshape(P, P)

    swap = np.arange(P) ^ (D // 2)
    proj = {
        "L0q": f["L0_xattn_Wq"].T, "L0k": f["L0_xattn_Wk"].T, "L0v": f["L0_xattn_Wv"].T, "L0o": f["L0_xattn_Wo"].T,
        "L1q": f["L1_xattn_Wq"], "L1k": f["L1_xattn_Wk"], "L1v": f["L1_xattn_Wv"], "L1o": f["L1_xattn_Wo"],
        "L2q1": heads(f["L2_xattn_Wq1"]), "L2k1": heads(f["L2_xattn_Wk1"]), "L2v1": heads(f["L2_xattn_Wv1"]),
        "L2q2": heads(f["L2_xattn_Wq2"]), "L2k2": heads(f["L2_xattn_Wk2"]), "L2v2": heads(f["L2_xattn_Wv2"]),
        "L3q": f["L3_xattn_q_w"].T, "L3qs": f["L3_xattn_q_w"].T[:, swap], "L3k": f["L3_xattn_k_w"].T,
        "L3ks": f["L3_xattn_k_w"].T[:, swap], "L3v": f["L3_xattn_v_w"].T, "L3o": f["L3_xattn_o_w"].T}
    for e in range(NE):
        for m in "qkvo":
            proj[f"E{m}{e}"] = f[f"L2_ffn_{m}W"][e].T
    col = {"L0q": f["L0_xattn_bq"], "L0k": f["L0_xattn_bk"], "L1q": f["L1_xattn_bq"], "L1k": f["L1_xattn_bk"],
           "L3q": f["L3_xattn_q_b"], "L3qs": f["L3_xattn_q_b"][swap], "L3k": f["L3_xattn_k_b"],
           "L3ks": f["L3_xattn_k_b"][swap]}
    for e in range(NE):
        col[f"Eq{e}"], col[f"Ek{e}"] = f["L2_ffn_qb"][e], f["L2_ffn_kb"][e]
        for c in range(CH):
            col[f"b1{e}{c}"] = f["L1_ffn_b1"][e, c * P:(c + 1) * P]
    for c in range(CH):
        col[f"f1{c}"] = f["L2_xattn_bf1"][c * P:(c + 1) * P]
    row = {"L0v": f["L0_xattn_bv"], "L0o": f["L0_xattn_bo"], "L1v": f["L1_xattn_bv"], "L1o": f["L1_xattn_bo"],
           "L2v1": f["L2_xattn_bv1"].reshape(P), "L2v2": f["L2_xattn_bv2"].reshape(P), "L3v": f["L3_xattn_v_b"],
           "L3o": f["L3_xattn_o_b"], "bf2": f["L2_xattn_bf2"]}
    for n in "123":
        row["g" + n], row["be" + n] = f["L2_xattn_g" + n], f["L2_xattn_be" + n]
    for e in range(NE):
        row[f"Ev{e}"] = f["L2_ffn_vb"][e]

    def down(w, chunks):
        return w.reshape(-1, chunks, P, P).transpose(2, 0, 1, 3).reshape(P, -1)

    a = {
        "x": f["x"], "ctx": f["ctx_1024"],
        "wproj": np.stack([proj[n] for n in PROJ], 1), "cols": np.stack([col[n] for n in COLS], 1),
        "rows": np.stack([row[n] for n in ROWS], 0),
        "w1_0": f["L0_ffn_w1"].transpose(2, 0, 1).reshape(P, -1), "w2_0": down(f["L0_ffn_w2"].transpose(0, 2, 1), CH),
        "w1_1": f["L1_ffn_W1"].transpose(2, 0, 1).reshape(P, -1), "w2_1": down(f["L1_ffn_W2"].transpose(0, 2, 1), CH),
        "gate_3": f["L3_ffn_kernel_gating_EDF"].transpose(1, 0, 2).reshape(P, -1),
        "up_3": f["L3_ffn_kernel_up_EDF"].transpose(1, 0, 2).reshape(P, -1),
        "down_3": down(f["L3_ffn_kernel_down_EFD"], CH3),
        "wf1": f["L2_xattn_Wf1"], "wf2": down(f["L2_xattn_Wf2"], CH),
        "router": np.stack([f["L0_ffn_gate_w"].T, f["L1_ffn_Wr"].T, f["L3_ffn_router_kernel_DE"]], 1),
        "rw1": f["L2_ffn_rW1"].T, "rw2": f["L2_ffn_rW2"].T,
        "rrow": np.stack([f["L2_ffn_rb1"], f["L2_ffn_ln_g"], f["L2_ffn_ln_b"]], 0), "rb2": f["L2_ffn_rb2"],
        "ebias": np.stack([f["L1_ffn_b2"], f["L2_ffn_ob"]], 1),
    }
    angle = (np.arange(P, dtype=np.float32)[None, :]
             * (1.0 / np.float32(10000.0) ** (np.arange(D // 2, dtype=np.float32) / (D // 2)))[np.arange(P) % (D // 2), None])
    sign = np.where(np.arange(P) % D < D // 2, -1.0, 1.0)[:, None]
    a["rope"] = np.stack([np.cos(angle), np.sin(angle) * sign], 1).astype(np.float32)
    one = np.eye(P, dtype=np.float32)
    a["ident"] = one
    q, k = np.arange(P)[:, None], np.arange(P)[None, :]
    causal, window = k <= q, (k <= q) & (k >= q - WINDOW)
    a["masks"] = np.stack([np.where(m, 0.0, NEG) for m in (causal, causal.T, window, window.T)], 1).astype(np.float32)
    a["band"] = (np.arange(P)[:, None] % 32 // D == np.arange(HB)[None, :]).astype(np.float32)
    a["tri"] = (np.arange(NE)[None, :] < np.arange(NE)[:, None]).astype(np.float32)
    return {n: np.ascontiguousarray(v) for n, v in a.items()}


def kernel(**inputs):
    import concourse.bacc as bacc
    from concourse.bass_utils import run_bass_kernel_spmd as run

    arrays = laid_out(inputs)

    def program(totals):
        nc = bacc.Bacc("TRN2", target_bir_lowering=False, num_devices=1)
        A = {n: nc.dram_tensor(f"in_{n}", a.shape, mybir.dt.from_np(a.dtype), kind="ExternalInput").ap()
             for n, a in arrays.items()}
        out = nc.dram_tensor("out_x", (NSEQ, P, P), F32, kind="ExternalOutput").ap()
        return nc, totals_of(build(nc, A, out, totals))

    _, totals = program({})
    nc, again = program(totals)
    assert again == totals
    r = run(nc, [{f"in_{n}": a for n, a in arrays.items()}], core_ids=[0])
    return r.results[0]["out_x"]
```

```python
from contextlib import ExitStack

import numpy as np

import concourse.bass as bass
from concourse import mybir

F32 = mybir.dt.float32
BF16 = mybir.dt.bfloat16
ALU = mybir.AluOpType
ACT = mybir.ActivationFunctionType
AX = mybir.AxisListType

P = 128
NSEQ = 32
NB = 4
GROUPS = NSEQ // NB
NT = NB * P
H = 16
D = P // H
BANDS = 4
HB = H // BANDS
NE = 8
SCALE = float(D) ** -0.5
EPS = 1e-5
WINDOW = 64
NORMS = 12
NEG = -1e30
TURNS = [BANDS * b + 8 for b in range(NB - 1)] + [NB * BANDS + 3]
STEPS = NB * BANDS + 4
LEAD = 2
CONSTS = 10
CH = 4
CH3 = 2


class Tally:

    def __init__(self, totals, base):
        self.totals, self.base, self.n = totals, base, {}

    def next(self, name, k=1):
        self.n[name] = self.n.get(name, 0) + k
        return self.at(name, self.n[name])

    def at(self, name, n):
        return self.base * self.totals.get(name, 0) + n


class Ring:

    def __init__(self, tally, name, banks):
        self.tally, self.name, self.banks, self.used = tally, name, banks, []
        self.count = {"act": 0, "dve": 0}

    def fill(self, consumer):
        n = len(self.used)
        self.count[consumer] += 1
        self.used.append((consumer, self.count[consumer]))
        old = self.taken(n - len(self.banks)) if n >= len(self.banks) else None
        return self.banks[n % len(self.banks)], self.tally.at(f"{self.name}_filled", n + 1), self.taken(n), old

    def taken(self, n):
        who, count = self.used[n]
        name = f"{self.name}_taken_{who}"
        return name, self.tally.at(name, count)


RINGS = {"s1": (0, 1), "s2": (2, 3), "o": (4, 5), "g": (6, 7)}
SIGNALS = [f"{r}_{s}" for r in RINGS for s in ("filled", "taken_act", "taken_dve")] + [
    "ln_ready",
    "split_ready",
    "zoned",
    "weighed",
    "r_ready",
    "router_in",
    "router_exp",
    "wts_ready",
    "var_ready",
    "rstd_ready",
    "out_ready",
    "dve_step"]

PROJ = ["L0q", "L0k", "L0v", "L0o", "L1q", "L1k", "L1v", "L1o", "L2q1", "L2k1", "L2v1", "L2q2", "L2k2",
        "L2v2", "L3q", "L3qs", "L3k", "L3ks", "L3v", "L3o"] + [f"E{m}{e}" for e in range(NE) for m in "qkvo"]
COLS = ["L0q", "L0k", "L1q", "L1k", "L3q", "L3qs", "L3k", "L3ks"] + [f"E{m}{e}" for e in range(NE) for m in "qk"] \
    + [f"f1{c}" for c in range(CH)] + [f"b1{e}{c}" for e in range(NE) for c in range(CH)]
ROWS = ["L0v", "L0o", "L1v", "L1o", "L2v1", "L2v2", "L3v", "L3o", "g1", "be1", "g2", "be2", "g3", "be3",
        "bf2"] + [f"Ev{e}" for e in range(NE)]


def build(nc, A, out, totals):
    with ExitStack() as ctx:
        def sb(name, shape, dt=F32):
            return ctx.enter_context(nc.sbuf_tensor(name, shape, dt))

        sem = {n: ctx.enter_context(nc.semaphore(n)) for n in SIGNALS}
        weights_in = ctx.enter_context(nc.semaphore("weights_in"))
        x_in = ctx.enter_context(nc.semaphore("x_in"))
        stored = ctx.enter_context(nc.semaphore("stored"))
        consts_set = ctx.enter_context(nc.semaphore("consts_set"))
        bank = [ctx.enter_context(nc.psum_tensor(f"bank{i}", [P, 512], F32)) for i in range(8)]

        wproj = sb("wproj", [P, len(PROJ), P])
        wf = {n: sb(n, [P, s]) for n, s in (("w1_0", NE * 512), ("w2_0", NE * CH * P), ("w1_1", NE * 512),
                                           ("w2_1", NE * CH * P), ("gate_3", NE * 256), ("up_3", NE * 256),
                                           ("down_3", NE * CH3 * P), ("wf1", 512), ("wf2", CH * P))}
        router = sb("router", [P, 3, NE])
        rw1 = sb("rw1", [P, P // 2])
        rw2 = sb("rw2", [P // 2, NE])
        cols = sb("cols", [P, len(COLS)])
        rows = sb("rows", [P, len(ROWS), P])
        rrow = sb("rrow", [P, 3, P // 2])
        rb2 = sb("rb2", [P, NE])
        ebias = sb("ebias", [NE, 2, P])
        rope = sb("rope", [P, 2, P])
        ident = sb("ident", [P, P])
        identb = sb("identb", [P, 2, P], BF16)
        masks = sb("masks", [P, 4, P], BF16)
        band = sb("band", [P, HB])
        tri = sb("tri", [P, NE, NE])

        x_tok = sb("x_tok", [P, NB, P])
        out_tok = sb("out_tok", [P, NB, P])
        h_tok = sb("h_tok", [P, NB, P])
        hh_tok = out_tok
        ctxT = sb("ctxT", [P, NT])
        hT = sb("hT", [P, NT])
        stats = sb("stats", [P, NB, 6])
        mv = sb("mv", [P, NB, 2])
        rstd = sb("rstd", [P, NB])
        power = sb("power", [P, NB])
        hid = sb("hid", [P, 2, CH, NT])
        sg = sb("sg", [P, 2, NT])
        qs = sb("qs", [P, NT])
        ks = sb("ks", [P, NT])
        spare = hid[:].rearrange("p a c n -> p (a c n)")
        qf = [sb("qf", [P, NT])[:], spare[:, 0:NT]]
        kf = [sb("kf", [P, NT])[:], spare[:, NT:2 * NT]]
        qm = [sb("qm", [P, HB, NT])[:], spare[:, 2 * NT:6 * NT].rearrange("p (i n) -> p i n", i=HB)]
        km = [sb("km", [P, HB, NT], BF16)[:],
              spare[:, 6 * NT:8 * NT].bitcast(BF16).rearrange("p (i n) -> p i n", i=HB)]
        qb = [sb("qb", [P, NT], BF16)[:], sg[:, 1, 0:NT // 2].bitcast(BF16)]
        kz = sb("kz", [P, 2, BANDS, P])
        qz = sb("qz", [P, 2, BANDS, P], BF16)
        vaug = sb("vaug", [P, 2, NB, H, D + 1])
        oT = [qs, ks]
        mx = sb("mx", [P, NB, H], BF16)
        ex = sb("ex", [P, 2, HB, P])
        rden = sb("rden", [P, NB, H])
        att_tok = sb("att_tok", [P, NB, P])
        c_st = att_tok
        attT = sb("attT", [P, NT])
        logit = sb("logit", [P, NB, NE])
        lmax = sb("lmax", [P, NB])
        cmp1, cmp2 = (ex[:, n, 0:2, :].rearrange("p i q -> p (i q)").rearrange("p (b e f) -> p b e f", b=NB, e=NE)
                      for n in range(2))
        top = sb("top", [P, NB, NE])
        lex = sb("lex", [P, NB, NE])
        wts = sb("wts", [P, NB, NE])
        wtsT = attT[0:NE, :]
        lsum = sb("lsum", [P, NB])
        r_full = sg[:, 0, :].rearrange("p (b f) -> p b f", b=NB)
        r_tok = r_full[:, :, 0:P // 2]
        rT = qs[0:P // 2, :]

        loads = [(wproj, A["wproj"]), (router, A["router"]), (rw1, A["rw1"]), (rw2, A["rw2"]), (cols, A["cols"]),
                 (rope, A["rope"]), (ident, A["ident"]),
                 (band, A["band"]), (ebias, A["ebias"])] + [(wf[n], A[n]) for n in wf]
        spread = [(rows, A["rows"]), (rrow, A["rrow"]), (rb2, A["rb2"]), (tri, A["tri"])]
        masks_f32 = hid[:, 0, 0, :].rearrange("p (m k) -> p m k", m=4)
        n_loads = len(loads) + len(spread) + 1

        x_dram = A["x"].rearrange("(g b) t f -> g t b f", b=NB)
        c_dram = A["ctx"].rearrange("(g b) t f -> g t b f", b=NB)
        o_dram = out.rearrange("(g b) t f -> g t b f", b=NB)

        def W(name):
            return wproj[:, PROJ.index(name), :]

        def col(name):
            return cols[:, COLS.index(name):COLS.index(name) + 1]

        def over_seqs(ap):
            return ap.unsqueeze(1).to_broadcast([P, NB, ap.shape[1]])

        def row(name):
            return over_seqs(rows[:, ROWS.index(name), :])

        def b4(ap):
            return ap.rearrange("p (b t) -> p b t", b=NB)

        block = ctx.enter_context(nc.Block())
        counted = {}

        @block.sync
        def _(sp):
            for dst, src in loads:
                sp.dma_start(dst[:], src).then_inc(weights_in, 16)
            sp.dma_start(masks_f32, A["masks"]).then_inc(weights_in, 16)
            for dst, src in spread:
                sp.dma_start(dst[:], src.unsqueeze(0).to_broadcast(list(dst.shape))).then_inc(weights_in, 16)
            with sp.Fori(0, GROUPS) as g:
                sp.wait_ge(sem["out_ready"], g)
                sp.dma_start(x_tok[:], x_dram[g]).then_inc(x_in, 16)
                sp.dma_start(c_st[:], c_dram[g]).then_inc(x_in, 16)

        @block.gpsimd
        def _(pool):
            pool.memset(vaug[:], 1.0).then_inc(consts_set, 1)
            pool.memset(kz[:], 0.0).then_inc(consts_set, 1)
            pool.memset(qz[:], 0.0).then_inc(consts_set, 1)
            pool.memset(power[:], -0.5).then_inc(consts_set, 1)
            pool.memset(sg[:], 0.0).then_inc(consts_set, 1)
            pool.wait_ge(consts_set, CONSTS)
            with pool.Fori(0, GROUPS) as g:
                t = Tally(totals, g)
                for _ in range(NORMS):
                    pool.wait_ge(sem["var_ready"], t.next("var_ready"))
                    nc.gpsimd.tensor_tensor(rstd[:], rstd[:], power[:], ALU.pow).then_inc(sem["rstd_ready"], 1)
                pool.wait_ge(sem["out_ready"], g + 1)
                pool.dma_start(o_dram[g], out_tok[:]).then_inc(stored, 16)
            pool.wait_ge(stored, 16 * GROUPS)

        @block.tensor
        def _(pe):
            pe.wait_ge(weights_in, 16 * n_loads)
            pe.wait_ge(consts_set, CONSTS)
            with pe.Fori(0, GROUPS) as g:
                t = Tally(totals, g)
                ring = {n: Ring(t, n, b) for n, b in RINGS.items()}
                pe.wait_ge(sem["out_ready"], g)

                def open_bank(name, consumer):
                    b, _, taken, old = ring[name].fill(consumer)
                    if old:
                        pe.wait_ge(sem[old[0]], old[1])
                    return bank[b], taken

                def wait_taken(taken):
                    pe.wait_ge(sem[taken[0]], taken[1])

                def to_T(src, ready, rows_=P, wait=True):
                    pe.wait_ge(sem[ready[0]], ready[1])
                    ps, taken = open_bank("g", "act")
                    for b in range(NB):
                        mm = nc.tensor.transpose(ps[0:rows_, b * P:(b + 1) * P], src[:, b, :], ident[:])
                    mm.then_inc(sem["g_filled"], 1)
                    if wait:
                        wait_taken(taken)
                    return taken

                def project(w, src):
                    ps, taken = open_bank("g", "act")
                    nc.tensor.matmul(ps[:], w, src[:], start=True, stop=True).then_inc(sem["g_filled"], 1)
                    return taken

                def by_token(w, src, n, k=P):
                    ps, taken = open_bank("g", "dve")
                    for b in range(NB):
                        mm = nc.tensor.matmul(ps[:, b * n:(b + 1) * n], src[0:k, b * P:(b + 1) * P], w,
                                              start=True, stop=True)
                    mm.then_inc(sem["g_filled"], 1)
                    return taken

                def prepare_q(slot, q, srcT, rot=False):
                    project(W(q), srcT)
                    if rot:
                        project(W(q + "s"), srcT)

                prepare_k = prepare_q

                def attend(slot, mask, between={}):
                    pe.wait_ge(sem["split_ready"], t.next("split_ready"))
                    units = [(b, j) for b in range(NB) for j in range(BANDS)]
                    o_bank, max_taken, exp_taken = {}, {}, {}

                    def scores(b, j):
                        s = slice(b * P, (b + 1) * P)
                        ps, max_taken[b, j] = open_bank("s1", "dve")
                        pe.wait_ge(sem["zoned"], t.next("zoned"))
                        mm = nc.tensor.matmul(ps[:], qz[:, b % 2, j, :], km[slot][:, :, s], start=True, stop=mask is None)
                        if mask is not None:
                            mm = nc.tensor.matmul(ps[:], identb[:, 0, :], masks[:, 2 * mask, :].unsqueeze(1)
                                                  .to_broadcast([P, HB, P]), start=False, stop=True)
                        mm.then_inc(sem["s1_filled"], 1)

                    def scores_t(b, j):
                        s = slice(b * P, (b + 1) * P)
                        ps, exp_taken[b, j] = open_bank("s2", "act")
                        nc.tensor.matmul(ps[:], kz[:, b % 2, j, :], qm[slot][:, :, s], start=True, stop=False)
                        if mask is not None:
                            nc.tensor.matmul(ps[:], identb[:, 0, :], masks[:, 2 * mask + 1, :].unsqueeze(1)
                                             .to_broadcast([P, HB, P]), start=False, stop=False)
                        wait_taken(max_taken[b, j])
                        for i in range(HB):
                            h = HB * j + i
                            mm = nc.tensor.matmul(ps[:, i * P:(i + 1) * P], mx[:, b, h:h + 1].to_broadcast([P, P]),
                                                  identb[:, 1, :], start=False, stop=i == HB - 1)
                        mm.then_inc(sem["s2_filled"], 1)

                    def weigh(n, b, j):
                        if j == 0:
                            o_bank[b] = open_bank("o", "act")
                        wait_taken(exp_taken[b, j])
                        for i in range(HB):
                            mm = nc.tensor.matmul(o_bank[b][0][32 * i:32 * i + D + 1, j * P:(j + 1) * P],
                                                  vaug[:, slot, b, HB * j + i, :], ex[:, n % 2, i, :],
                                                  start=True, stop=True)
                        mm.then_inc(sem["weighed"], 1)

                    def turn(b):
                        wait_taken(o_bank[b][1])
                        ps, taken = open_bank("g", "dve")
                        for j in range(BANDS):
                            mm = nc.tensor.transpose(ps[:, j * P:(j + 1) * P], oT[b % 2][:, j * P:(j + 1) * P], ident[:])
                        mm.then_inc(sem["g_filled"], 1)
                        return taken

                    for n in range(STEPS):
                        if n < len(units):
                            scores(*units[n])
                        if 1 <= n <= len(units):
                            scores_t(*units[n - 1])
                        if 2 <= n < len(units) + 2:
                            weigh(n - 2, *units[n - 2])
                        for other in between.get(n, []):
                            other()
                        if n in TURNS:
                            taken = turn(TURNS.index(n))
                    return taken

                def attention(q, k, v, srcT, kvT, mask, rot=False):
                    prepare_q(0, q, srcT, rot)
                    prepare_k(0, k, kvT, rot)
                    by_token(W(v), kvT, P)
                    return attend(0, mask)

                def out_proj(w, attended):
                    to_T(att_tok, attended)
                    by_token(w, attT, P)

                def experts(w1, w2, chunks, kinds):
                    taken = {}

                    def first(e):
                        for c in range(chunks):
                            for w, who in zip(w1, kinds):
                                ps, taken[e] = open_bank("s1", who)
                                at = (e * chunks + c) * P
                                nc.tensor.matmul(ps[:], w[:, at:at + P], hT[:], start=True, stop=True)\
                                    .then_inc(sem["s1_filled"], 1)

                    def second(e):
                        wait_taken(taken[e])
                        ps, _ = open_bank("s2", "dve")
                        for b in range(NB):
                            for c in range(chunks):
                                at = (e * chunks + c) * P
                                mm = nc.tensor.matmul(ps[:, b * P:(b + 1) * P], hid[:, e % 2, c, b * P:(b + 1) * P],
                                                      w2[:, at:at + P], start=c == 0, stop=c == chunks - 1)
                        mm.then_inc(sem["s2_filled"], 1)
                    return first, second

                def mixture(w1, w2, chunks, kinds):
                    first, second = experts(w1, w2, chunks, kinds)
                    for e in range(NE + 1):
                        if e < NE:
                            first(e)
                        if e:
                            second(e - 1)

                def expert_biases(k):
                    to_T(wts, ("wts_ready", t.next("wts_ready")), NE)
                    by_token(ebias[:, k, :], wtsT, P, NE)

                def to_hT():
                    to_T(h_tok, ("ln_ready", t.next("ln_ready")))

                pe.wait_ge(x_in, g * 32 + 32)
                ps, taken = open_bank("g", "act")
                for b in range(NB):
                    mm = nc.tensor.transpose(ps[:, b * P:(b + 1) * P], c_st[:, b, :], ident[:])
                mm.then_inc(sem["g_filled"], 1)
                wait_taken(taken)
                to_hT()
                out_proj(W("L0o"), attention("L0q", "L0k", "L0v", hT, ctxT, 0))
                to_hT()
                by_token(router[:, 0, :], hT, NE)
                mixture([wf["w1_0"]], wf["w2_0"], CH, ["act"])
                to_hT()
                out_proj(W("L1o"), attention("L1q", "L1k", "L1v", hT, ctxT, None))
                to_hT()
                by_token(router[:, 1, :], hT, NE)
                mixture([wf["w1_1"]], wf["w2_1"], CH, ["act"])
                expert_biases(0)
                to_hT()
                attention("L2q1", "L2k1", "L2v1", hT, hT, 0)
                to_hT()
                attention("L2q2", "L2k2", "L2v2", hT, ctxT, None)
                to_hT()
                first, second = experts([wf["wf1"]], wf["wf2"], CH, ["act"])
                first(0)
                second(0)
                to_hT()
                by_token(rw1[:], hT, P // 2)
                to_T(r_full, ("r_ready", t.next("r_ready")))
                by_token(rw2[:], rT, NE, P // 2)
                prepare_q(0, "Eq0", hT)
                prepare_k(0, "Ek0", hT)
                by_token(W("Ev0"), hT, P)
                attended, turned = None, None

                def turn_last():
                    nonlocal turned
                    turned = to_T(att_tok, attended, wait=False)

                for e in range(NE):
                    between = {}
                    if e:
                        between[1] = [turn_last]
                        between[3] = [lambda: (wait_taken(turned), by_token(W(f"Eo{e - 1}"), attT, P))]
                    if e + 1 < NE:
                        between[4] = [lambda: prepare_q((e + 1) % 2, f"Eq{e + 1}", hT)]
                        between[5] = [lambda: prepare_k((e + 1) % 2, f"Ek{e + 1}", hT)]
                        between[6] = [lambda: by_token(W(f"Ev{e + 1}"), hT, P)]
                    attended = attend(e % 2, None, between)
                out_proj(W(f"Eo{NE - 1}"), attended)
                expert_biases(1)
                to_hT()
                out_proj(W("L3o"), attention("L3q", "L3k", "L3v", hT, ctxT, 1, True))
                to_hT()
                by_token(router[:, 2, :], hT, NE)
                mixture([wf["gate_3"], wf["up_3"]], wf["down_3"], CH3, ["act", "dve"])
            counted["pe"] = (t, ring)

        @block.scalar
        def _(act):
            act.wait_ge(weights_in, 16 * n_loads)
            act.wait_ge(consts_set, CONSTS)
            with act.Fori(0, GROUPS) as g:
                t = Tally(totals, g)
                ring = {n: Ring(t, n, b) for n, b in RINGS.items()}

                def take(name):
                    b, full, _, _ = ring[name].fill("act")
                    act.wait_ge(sem[name + "_filled"], full)
                    return bank[b]

                def skip(name, n=1):
                    for _ in range(n):
                        taken = ring[name].fill("dve")[2]
                    return taken

                def evacuate(dst, parts=P):
                    ps = take("g")
                    nc.scalar.activation(dst, ps[0:parts, :], ACT.Copy).then_inc(sem["g_taken_act"], 1)

                def prepare(slot, dsts, name, bias):
                    ps = take("g")
                    for dst in dsts:
                        if bias:
                            ins = nc.scalar.activation(dst, ps[:], ACT.Identity, bias=col(name))
                        else:
                            ins = nc.scalar.activation(dst, ps[:], ACT.Copy)
                    ins.then_inc(sem["g_taken_act"], 1)

                def prepare_q(slot, name, bias, rot=False):
                    prepare(slot, [qf[slot]] if rot else [qb[slot], qf[slot]], name, bias)
                    if rot:
                        prepare(slot, [qs[:]], name + "s", bias)

                def prepare_k(slot, name, bias, rot=False):
                    prepare(slot, [kf[slot]], name, bias)
                    if rot:
                        prepare(slot, [ks[:]], name + "s", bias)

                def attend(between={}):
                    for n in range(STEPS):
                        if 1 <= n <= NB * BANDS:
                            skip("s1")
                            ps = take("s2")
                            before = t.n.get("weighed", 0)
                            if before >= 2:
                                act.wait_ge(sem["weighed"], t.at("weighed", before - 1))
                            t.next("weighed")
                            ins = nc.scalar.activation(ex[:, (n - 1) % 2, :, :],
                                                       ps[:].rearrange("p (i q) -> p i q", i=HB),
                                                       ACT.Exp, scale=SCALE)
                            ins.then_inc(sem["s2_taken_act"], 1)
                        for other in between.get(n, []):
                            other()
                        if n + 1 in TURNS:
                            b = TURNS.index(n + 1)
                            b_, _, taken, _ = ring["o"].fill("act")
                            done = t.n["weighed"] - min(n, NB * BANDS) + BANDS * (b + 1)
                            act.wait_ge(sem["weighed"], t.at("weighed", done))
                            if b >= 2:
                                act.wait_ge(sem[turned[b - 2][0]], turned[b - 2][1])
                            nc.scalar.activation(oT[b % 2][:], bank[b_][:], ACT.Copy).then_inc(sem[taken[0]], 1)
                        if n in TURNS:
                            b = TURNS.index(n)
                            if b == 0:
                                turned = {}
                            turned[b] = skip("g")

                def attention(bias, q, k, rot=False):
                    prepare_q(0, q, bias, rot)
                    prepare_k(0, k, bias, rot)
                    skip("g")
                    attend()

                def out_proj():
                    evacuate(attT[:])
                    skip("g")

                def gates(times=1):
                    skip("g")
                    for _ in range(times):
                        act.wait_ge(sem["router_in"], t.next("router_in"))
                        nc.scalar.activation(lex[:], logit[:], ACT.Exp)\
                            .then_inc(sem["router_exp"], 1)

                def mixture(func, ne, biases=None):
                    for e in range(ne):
                        for c in range(CH):
                            ps = take("s1")
                            kw = {"bias": col(biases(e, c))} if biases else {}
                            ins = nc.scalar.activation(hid[:, e % 2, c, :], ps[:], func, **kw)
                            ins.then_inc(sem["s1_taken_act"], 1)
                        skip("s2")

                def expert_biases():
                    evacuate(wtsT, NE)
                    skip("g")

                evacuate(ctxT[:])
                evacuate(hT[:])
                attention(True, "L0q", "L0k")
                out_proj()
                evacuate(hT[:])
                gates()
                mixture(ACT.Relu, NE)
                evacuate(hT[:])
                attention(True, "L1q", "L1k")
                out_proj()
                evacuate(hT[:])
                gates()
                mixture(ACT.Gelu, NE, lambda e, c: f"b1{e}{c}")
                expert_biases()
                evacuate(hT[:])
                attention(False, "L2q1", "L2k1")
                evacuate(hT[:])
                attention(False, "L2q2", "L2k2")
                evacuate(hT[:])
                mixture(ACT.Relu, 1, lambda e, c: f"f1{c}")
                evacuate(hT[:])
                skip("g")
                evacuate(rT[:], P // 2)
                gates()
                prepare_q(0, "Eq0", True)
                prepare_k(0, "Ek0", True)
                skip("g")
                for e in range(NE):
                    between = {}
                    if e:
                        between[2] = [lambda: evacuate(attT[:])]
                        between[3] = [lambda: skip("g")]
                    if e + 1 < NE:
                        between[5] = [lambda: prepare_q((e + 1) % 2, f"Eq{e + 1}", True)]
                        between[6] = [lambda: prepare_k((e + 1) % 2, f"Ek{e + 1}", True), lambda: skip("g")]
                    attend(between)
                out_proj()
                expert_biases()
                evacuate(hT[:])
                attention(True, "L3q", "L3k", True)
                out_proj()
                evacuate(hT[:])
                gates(2)
                multiplied = []
                for e in range(NE):
                    for c in range(CH3):
                        ps = take("s1")
                        multiplied.append(ring["s1"].fill("dve")[2])
                        n = e * CH3 + c
                        if n >= 2:
                            act.wait_ge(sem[multiplied[n - 2][0]], multiplied[n - 2][1])
                        nc.scalar.activation(sg[:, n % 2, :], ps[:], ACT.Silu).then_inc(sem["s1_taken_act"], 1)
                    skip("s2")
            counted["act"] = (t, ring)

        @block.vector
        def _(dve):
            dve.wait_ge(weights_in, 16 * n_loads)
            nc.vector.memset(bank[RINGS["o"][0]][:], 0.0).then_inc(consts_set, 1)
            nc.vector.memset(bank[RINGS["o"][1]][:], 0.0).then_inc(consts_set, 1)
            nc.vector.tensor_copy(masks[:], masks_f32).then_inc(consts_set, 1)
            nc.vector.tensor_copy(identb[:, 0, :], ident[:]).then_inc(consts_set, 1)
            nc.vector.tensor_scalar(identb[:, 1, :], ident[:], -1.0, None, ALU.mult).then_inc(consts_set, 1)
            dve.wait_ge(consts_set, CONSTS)
            with dve.Fori(0, GROUPS) as g:
                t = Tally(totals, g)
                ring = {n: Ring(t, n, b) for n, b in RINGS.items()}

                def settle(ins, name="dve_step"):
                    ins.then_inc(sem[name], 1)
                    dve.wait_ge(sem[name], t.next(name))

                def settle_taken(ins, taken):
                    ins.then_inc(sem[taken[0]], 1)
                    dve.wait_ge(sem[taken[0]], taken[1])

                def take(name):
                    b, full, taken, _ = ring[name].fill("dve")
                    dve.wait_ge(sem[name + "_filled"], full)
                    return bank[b], taken

                def skip(name, n=1):
                    for _ in range(n):
                        taken = ring[name].fill("act")[2]
                    return taken

                def normalize(src, dst, n=P, gain=None, shift=None, relu=False):
                    for b in range(NB):
                        ins = nc.vector.bn_stats(stats[:, b, :], src[:, b, :])
                    settle(ins)
                    nc.vector.memset(rstd[:], 0.0)
                    for b in range(NB):
                        ins = nc.vector.bn_aggr(mv[:, b, :], stats[:, b, :])
                    settle(ins)
                    nc.vector.tensor_scalar(rstd[:], mv[:, :, 1], EPS, None, ALU.add)\
                        .then_inc(sem["var_ready"], 1)
                    t.next("var_ready")
                    dve.wait_ge(sem["rstd_ready"], t.next("rstd_ready"))
                    for b in range(NB):
                        ins = nc.vector.tensor_scalar(dst[:, b, :], src[:, b, :], mv[:, b, 0:1], rstd[:, b:b + 1],
                                                      ALU.subtract, ALU.mult)
                    if gain is not None:
                        settle(ins)
                        settle(nc.vector.tensor_tensor(dst[:], dst[:], gain, ALU.mult))
                        ins = nc.vector.tensor_tensor(dst[:], dst[:], shift, ALU.add)
                        if relu:
                            settle(ins)
                            ins = nc.vector.tensor_scalar(dst[:], dst[:], 0.0, None, ALU.max)
                    return ins

                def norm_to_hT(src, **kw):
                    settle(normalize(src, h_tok, **kw), "ln_ready")
                    skip("g")

                def values(slot, v):
                    ps, taken = take("g")
                    for b in range(NB):
                        ins = nc.vector.tensor_tensor(vaug[:, slot, b, :, 0:D],
                                                      ps[:, b * P:(b + 1) * P].rearrange("p (h d) -> p h d", d=D),
                                                      rows[:, ROWS.index(v), :].rearrange("p (h d) -> p h d", d=D),
                                                      ALU.add)
                    ins.then_inc(sem[taken[0]], 1)

                def split_k(slot, projected, heads=range(HB)):
                    dve.wait_ge(sem[projected[0]], projected[1])
                    for i in heads:
                        ins = nc.vector.tensor_scalar(km[slot][:, i, :], kf[slot], band[:, i:i + 1], None, ALU.mult)
                    return ins

                def split_q(slot, heads=range(HB)):
                    for i in heads:
                        ins = nc.vector.tensor_scalar(qm[slot][:, i, :], qf[slot], band[:, i:i + 1], None, ALU.mult)
                    return ins

                def rotate(projected):
                    dve.wait_ge(sem[projected[0]], projected[1])
                    for a, s in ((qf[0], qs[:]), (kf[0], ks[:])):
                        nc.vector.tensor_tensor(b4(a), b4(a), over_seqs(rope[:, 0, :]), ALU.mult)
                        settle(nc.vector.tensor_tensor(b4(s), b4(s), over_seqs(rope[:, 1, :]), ALU.mult))
                        settle(nc.vector.tensor_tensor(a, a, s, ALU.add))
                    settle(nc.vector.tensor_copy(qb[0], qf[0]))

                def attend(slot=0, between={}):
                    def zone(b, j):
                        p, s = slice(32 * j, 32 * j + 32), slice(b * P, (b + 1) * P)
                        nc.vector.tensor_copy(qz[p, b % 2, j, :], qb[slot][p, s])
                        nc.vector.tensor_copy(kz[p, b % 2, j, :], kf[slot][p, s]).then_inc(sem["zoned"], 1)

                    def maximum(b, j):
                        ps, taken = take("s1")
                        ins = nc.vector.tensor_reduce(mx[:, b, HB * j:HB * j + HB],
                                                      ps[:].rearrange("p (i k) -> p i k", i=HB), AX.X, ALU.max)
                        ins.then_inc(sem[taken[0]], 1)
                        skip("s2")

                    def divide(b):
                        ps, taken = take("g")
                        o = ps[:].rearrange("p (h d) -> p h d", d=32)
                        settle(nc.vector.reciprocal(rden[:, b, :], o[:, :, D]))
                        ins = nc.vector.tensor_tensor(att_tok[:, b, :].rearrange("p (h d) -> p h d", d=D),
                                                      o[:, :, 0:D],
                                                      rden[:, b, :].unsqueeze(2).to_broadcast([P, H, D]), ALU.mult)
                        ins.then_inc(sem[taken[0]], 1)
                        return taken

                    for n in range(LEAD):
                        zone(n // BANDS, n % BANDS)
                    for n in range(STEPS):
                        if n + LEAD < NB * BANDS:
                            zone((n + LEAD) // BANDS, (n + LEAD) % BANDS)
                        if n < NB * BANDS:
                            maximum(n // BANDS, n % BANDS)
                        for other in between.get(n, []):
                            other()
                        if n in TURNS:
                            taken = divide(TURNS.index(n))
                    dve.wait_ge(sem[taken[0]], taken[1])

                def attention(v, rot=False):
                    projected = skip("g", 4 if rot else 2)
                    values(0, v)
                    if rot:
                        rotate(projected)
                    split_k(0, projected)
                    split_q(0).then_inc(sem["split_ready"], 1)
                    attend()

                def out_proj():
                    skip("g")
                    return take("g")

                def residual(bias):
                    ps, taken = out_proj()
                    settle_taken(nc.vector.tensor_tensor(x_tok[:], x_tok[:], b4(ps[:]), ALU.add), taken)
                    settle(nc.vector.tensor_tensor(x_tok[:], x_tok[:], row(bias), ALU.add))

                def gates(bias=False, twice=False):
                    ps, taken = take("g")
                    lg = ps[:, 0:NB * NE].rearrange("p (b e) -> p b e", b=NB)
                    if bias:
                        ins = nc.vector.tensor_tensor(logit[:], lg, over_seqs(rb2[:]), ALU.add)
                    else:
                        ins = nc.vector.tensor_copy(logit[:], lg)
                    settle_taken(ins, taken)
                    nc.vector.tensor_reduce(lmax[:], logit[:], AX.X, ALU.max)
                    for b in range(NB):
                        other = logit[:, b, :].unsqueeze(1).to_broadcast([P, NE, NE])
                        own = logit[:, b, :].unsqueeze(2).to_broadcast([P, NE, NE])
                        nc.vector.tensor_tensor(cmp1[:, b], other, own, ALU.is_gt)
                        ins = nc.vector.tensor_tensor(cmp2[:, b], other, own, ALU.is_equal)
                    settle(ins)
                    settle(nc.vector.tensor_tensor(cmp2, cmp2, tri[:].unsqueeze(1)
                                                   .to_broadcast([P, NB, NE, NE]), ALU.mult))
                    settle(nc.vector.tensor_tensor(cmp1, cmp1, cmp2, ALU.add))
                    settle(nc.vector.tensor_reduce(top[:], cmp1, AX.X, ALU.add))
                    nc.vector.tensor_scalar(top[:], top[:], 1.5, None, ALU.is_lt)
                    ins = nc.vector.tensor_tensor(logit[:], logit[:], lmax[:].unsqueeze(2).to_broadcast([P, NB, NE]),
                                                  ALU.subtract)
                    ins.then_inc(sem["router_in"], 1)
                    t.next("router_in")

                    def exped():
                        dve.wait_ge(sem["router_exp"], t.next("router_exp"))

                    def share(dst):
                        settle(nc.vector.tensor_reduce(lsum[:], dst[:], AX.X, ALU.add))
                        settle(nc.vector.reciprocal(lsum[:], lsum[:]))
                        return nc.vector.tensor_tensor(dst[:], dst[:], lsum[:].unsqueeze(2)
                                                       .to_broadcast([P, NB, NE]), ALU.mult)
                    exped()
                    if twice:
                        settle(share(lex))
                        ins = nc.vector.tensor_tensor(logit[:], lex[:], lsum[:].unsqueeze(2)
                                                      .to_broadcast([P, NB, NE]), ALU.subtract)
                        ins.then_inc(sem["router_in"], 1)
                        t.next("router_in")
                        exped()
                    settle(nc.vector.tensor_tensor(wts[:], lex[:], top[:], ALU.mult))
                    return share(wts)

                def add_weighted(took, e):
                    ps, taken = took
                    for b in range(NB):
                        ins = nc.vector.scalar_tensor_tensor(x_tok[:, b, :], ps[:, b * P:(b + 1) * P],
                                                             wts[:, b, e:e + 1], x_tok[:, b, :], ALU.mult, ALU.add)
                    settle_taken(ins, taken)

                def expert_biases():
                    skip("g")
                    ps, taken = take("g")
                    settle_taken(nc.vector.tensor_tensor(x_tok[:], x_tok[:], b4(ps[:]), ALU.add), taken)

                def mixture():
                    for e in range(NE):
                        skip("s1", CH)
                        add_weighted(take("s2"), e)

                dve.wait_ge(x_in, g * 32 + 32)
                skip("g")
                norm_to_hT(x_tok)
                attention("L0v")
                residual("L0o")
                norm_to_hT(x_tok)
                settle(gates())
                mixture()
                norm_to_hT(x_tok)
                attention("L1v")
                residual("L1o")
                norm_to_hT(x_tok)
                settle(gates(), "wts_ready")
                mixture()
                expert_biases()
                norm_to_hT(x_tok)
                attention("L2v1")
                dve.wait_ge(stored, g * 16)
                settle(nc.vector.tensor_tensor(hh_tok[:], h_tok[:], att_tok[:], ALU.add))
                norm_to_hT(hh_tok, gain=row("g1"), shift=row("be1"))
                attention("L2v2")
                settle(nc.vector.tensor_tensor(hh_tok[:], h_tok[:], att_tok[:], ALU.add))
                norm_to_hT(hh_tok, gain=row("g2"), shift=row("be2"))
                skip("s1", CH)
                ps, taken = take("s2")
                settle_taken(nc.vector.tensor_tensor(hh_tok[:], h_tok[:], b4(ps[:]), ALU.add), taken)
                settle(nc.vector.tensor_tensor(hh_tok[:], hh_tok[:], row("bf2"), ALU.add))
                settle(normalize(hh_tok, h_tok, gain=row("g3"), shift=row("be3")))
                settle(nc.vector.tensor_tensor(x_tok[:], x_tok[:], h_tok[:], ALU.add))
                norm_to_hT(x_tok)
                ps, taken = take("g")
                ins = nc.vector.tensor_tensor(r_tok, ps[:, 0:NB * P // 2].rearrange("p (b f) -> p b f", b=NB),
                                              over_seqs(rrow[:, 0, :]), ALU.add)
                settle_taken(ins, taken)
                normalize(r_tok, r_tok, gain=over_seqs(rrow[:, 1, :]), shift=over_seqs(rrow[:, 2, :]), relu=True)\
                    .then_inc(sem["r_ready"], 1)
                t.next("r_ready")
                skip("g")
                settle(gates(bias=True), "wts_ready")
                projected = skip("g", 2)
                values(0, "Ev0")
                split_k(0, projected)
                split_q(0).then_inc(sem["split_ready"], 1)
                for e in range(NE):
                    between = {}
                    if e:
                        between[2] = [lambda: skip("g")]
                        between[4] = [lambda: add_weighted(take("g"), e - 1)]
                    if e + 1 < NE:
                        slot = (e + 1) % 2
                        projected = []
                        between[6] = [lambda: projected.append(skip("g", 2))]
                        between[7] = [lambda: values(slot, f"Ev{e + 1}")]
                        for i in range(HB):
                            between.setdefault(9 + i, []).append(lambda i=i: split_k(slot, projected[0], [i]))
                        for i in range(HB - 1):
                            between[13 + i] = [lambda i=i: split_q(slot, [i])]
                        between[12 + HB] = [lambda: split_q(slot, [HB - 1]).then_inc(sem["split_ready"], 1)]
                    attend(e % 2, between)
                add_weighted(out_proj(), NE - 1)
                expert_biases()
                norm_to_hT(x_tok)
                attention("L3v", True)
                residual("L3o")
                norm_to_hT(x_tok)
                settle(gates(twice=True))

                def gate_hidden(e):
                    for c in range(CH3):
                        n = e * CH3 + c
                        silu = skip("s1")
                        dve.wait_ge(sem[silu[0]], silu[1])
                        ps, taken = take("s1")
                        ins = nc.vector.tensor_tensor(hid[:, e % 2, c, :], ps[:], sg[:, n % 2, :], ALU.mult)
                        ins.then_inc(sem[taken[0]], 1)

                for e in range(NE + 1):
                    if e < NE:
                        gate_hidden(e)
                    if e:
                        add_weighted(take("s2"), e - 1)
                nc.vector.tensor_copy(out_tok[:], x_tok[:]).then_inc(sem["out_ready"], 1)
                dve.wait_ge(sem["out_ready"], t.next("out_ready"))
            counted["dve"] = (t, ring)
    return counted


def totals_of(counted):
    got = {}
    for t, ring in counted.values():
        for name, n in t.n.items():
            got[name] = max(got.get(name, 0), n)
        for r in ring.values():
            assert r.name == "o" or got.get(f"{r.name}_filled", len(r.used)) == len(r.used), r.name
            got[f"{r.name}_filled"] = max(len(r.used), got.get(f"{r.name}_filled", 0))
            for who, n in r.count.items():
                got[f"{r.name}_taken_{who}"] = max(n, got.get(f"{r.name}_taken_{who}", 0))
    return got


def laid_out(i):
    f = {k: np.asarray(v) for k, v in i.items()}

    def heads(w):
        return w.transpose(1, 0, 2).reshape(P, P)

    swap = np.arange(P) ^ (D // 2)
    proj = {
        "L0q": f["L0_xattn_Wq"].T, "L0k": f["L0_xattn_Wk"].T, "L0v": f["L0_xattn_Wv"].T, "L0o": f["L0_xattn_Wo"].T,
        "L1q": f["L1_xattn_Wq"], "L1k": f["L1_xattn_Wk"], "L1v": f["L1_xattn_Wv"], "L1o": f["L1_xattn_Wo"],
        "L2q1": heads(f["L2_xattn_Wq1"]), "L2k1": heads(f["L2_xattn_Wk1"]), "L2v1": heads(f["L2_xattn_Wv1"]),
        "L2q2": heads(f["L2_xattn_Wq2"]), "L2k2": heads(f["L2_xattn_Wk2"]), "L2v2": heads(f["L2_xattn_Wv2"]),
        "L3q": f["L3_xattn_q_w"].T, "L3qs": f["L3_xattn_q_w"].T[:, swap], "L3k": f["L3_xattn_k_w"].T,
        "L3ks": f["L3_xattn_k_w"].T[:, swap], "L3v": f["L3_xattn_v_w"].T, "L3o": f["L3_xattn_o_w"].T}
    for e in range(NE):
        for m in "qkvo":
            proj[f"E{m}{e}"] = f[f"L2_ffn_{m}W"][e].T
    col = {"L0q": f["L0_xattn_bq"], "L0k": f["L0_xattn_bk"], "L1q": f["L1_xattn_bq"], "L1k": f["L1_xattn_bk"],
           "L3q": f["L3_xattn_q_b"], "L3qs": f["L3_xattn_q_b"][swap], "L3k": f["L3_xattn_k_b"],
           "L3ks": f["L3_xattn_k_b"][swap]}
    for e in range(NE):
        col[f"Eq{e}"], col[f"Ek{e}"] = f["L2_ffn_qb"][e], f["L2_ffn_kb"][e]
        for c in range(CH):
            col[f"b1{e}{c}"] = f["L1_ffn_b1"][e, c * P:(c + 1) * P]
    for c in range(CH):
        col[f"f1{c}"] = f["L2_xattn_bf1"][c * P:(c + 1) * P]
    row = {"L0v": f["L0_xattn_bv"], "L0o": f["L0_xattn_bo"], "L1v": f["L1_xattn_bv"], "L1o": f["L1_xattn_bo"],
           "L2v1": f["L2_xattn_bv1"].reshape(P), "L2v2": f["L2_xattn_bv2"].reshape(P), "L3v": f["L3_xattn_v_b"],
           "L3o": f["L3_xattn_o_b"], "bf2": f["L2_xattn_bf2"]}
    for n in "123":
        row["g" + n], row["be" + n] = f["L2_xattn_g" + n], f["L2_xattn_be" + n]
    for e in range(NE):
        row[f"Ev{e}"] = f["L2_ffn_vb"][e]

    def down(w, chunks):
        return w.reshape(-1, chunks, P, P).transpose(2, 0, 1, 3).reshape(P, -1)

    a = {
        "x": f["x"], "ctx": f["ctx_1024"],
        "wproj": np.stack([proj[n] for n in PROJ], 1), "cols": np.stack([col[n] for n in COLS], 1),
        "rows": np.stack([row[n] for n in ROWS], 0),
        "w1_0": f["L0_ffn_w1"].transpose(2, 0, 1).reshape(P, -1), "w2_0": down(f["L0_ffn_w2"].transpose(0, 2, 1), CH),
        "w1_1": f["L1_ffn_W1"].transpose(2, 0, 1).reshape(P, -1), "w2_1": down(f["L1_ffn_W2"].transpose(0, 2, 1), CH),
        "gate_3": f["L3_ffn_kernel_gating_EDF"].transpose(1, 0, 2).reshape(P, -1),
        "up_3": f["L3_ffn_kernel_up_EDF"].transpose(1, 0, 2).reshape(P, -1),
        "down_3": down(f["L3_ffn_kernel_down_EFD"], CH3),
        "wf1": f["L2_xattn_Wf1"], "wf2": down(f["L2_xattn_Wf2"], CH),
        "router": np.stack([f["L0_ffn_gate_w"].T, f["L1_ffn_Wr"].T, f["L3_ffn_router_kernel_DE"]], 1),
        "rw1": f["L2_ffn_rW1"].T, "rw2": f["L2_ffn_rW2"].T,
        "rrow": np.stack([f["L2_ffn_rb1"], f["L2_ffn_ln_g"], f["L2_ffn_ln_b"]], 0), "rb2": f["L2_ffn_rb2"],
        "ebias": np.stack([f["L1_ffn_b2"], f["L2_ffn_ob"]], 1),
    }
    angle = (np.arange(P, dtype=np.float32)[None, :]
             * (1.0 / np.float32(10000.0) ** (np.arange(D // 2, dtype=np.float32) / (D // 2)))[np.arange(P) % (D // 2), None])
    sign = np.where(np.arange(P) % D < D // 2, -1.0, 1.0)[:, None]
    a["rope"] = np.stack([np.cos(angle), np.sin(angle) * sign], 1).astype(np.float32)
    one = np.eye(P, dtype=np.float32)
    a["ident"] = one
    q, k = np.arange(P)[:, None], np.arange(P)[None, :]
    causal, window = k <= q, (k <= q) & (k >= q - WINDOW)
    a["masks"] = np.stack([np.where(m, 0.0, NEG) for m in (causal, causal.T, window, window.T)], 1).astype(np.float32)
    a["band"] = (np.arange(P)[:, None] % 32 // D == np.arange(HB)[None, :]).astype(np.float32)
    a["tri"] = (np.arange(NE)[None, :] < np.arange(NE)[:, None]).astype(np.float32)
    return {n: np.ascontiguousarray(v) for n, v in a.items()}


def kernel(**inputs):
    import concourse.bacc as bacc
    from concourse.bass_utils import run_bass_kernel_spmd as run

    arrays = laid_out(inputs)

    def program(totals):
        nc = bacc.Bacc("TRN2", target_bir_lowering=False, num_devices=1)
        A = {n: nc.dram_tensor(f"in_{n}", a.shape, mybir.dt.from_np(a.dtype), kind="ExternalInput").ap()
             for n, a in arrays.items()}
        out = nc.dram_tensor("out_x", (NSEQ, P, P), F32, kind="ExternalOutput").ap()
        return nc, totals_of(build(nc, A, out, totals))

    _, totals = program({})
    nc, again = program(totals)
    assert again == totals
    r = run(nc, [{f"in_{n}": a for n, a in arrays.items()}], core_ids=[0])
    return r.results[0]["out_x"]
```

```python
from contextlib import ExitStack

import numpy as np

import concourse.bass as bass
from concourse import mybir

F32 = mybir.dt.float32
BF16 = mybir.dt.bfloat16
ALU = mybir.AluOpType
ACT = mybir.ActivationFunctionType
AX = mybir.AxisListType

P = 128
NSEQ = 32
NB = 4
GROUPS = NSEQ // NB
NT = NB * P
H = 16
D = P // H
BANDS = 4
HB = H // BANDS
NE = 8
SCALE = float(D) ** -0.5
EPS = 1e-5
WINDOW = 64
NEG = -1e30
TURNS = [BANDS * b + 8 for b in range(NB - 1)] + [NB * BANDS + 3]
STEPS = NB * BANDS + 4
TAIL = {9: ["att0"], 10: ["out0"], 13: ["norm0", "att1"], 14: ["out1"], 17: ["norm1", "att2"], 18: ["out2"],
        20: ["att3"], 21: ["out3", "norm2"], 22: ["norm3"]}
LEAD = 2
CONSTS = 11
CH = 4
CH3 = 2


class Tally:

    def __init__(self, totals, base):
        self.totals, self.base, self.n = totals, base, {}

    def next(self, name, k=1):
        self.n[name] = self.n.get(name, 0) + k
        return self.at(name, self.n[name])

    def at(self, name, n):
        return self.base * self.totals.get(name, 0) + n


class Ring:

    def __init__(self, tally, name, banks):
        self.tally, self.name, self.banks, self.used = tally, name, banks, []
        self.count = {"act": 0, "dve": 0}

    def fill(self, consumer):
        n = len(self.used)
        self.count[consumer] += 1
        self.used.append((consumer, self.count[consumer]))
        old = self.taken(n - len(self.banks)) if n >= len(self.banks) else None
        return self.banks[n % len(self.banks)], self.tally.at(f"{self.name}_filled", n + 1), self.taken(n), old

    def taken(self, n):
        who, count = self.used[n]
        name = f"{self.name}_taken_{who}"
        return name, self.tally.at(name, count)


RINGS = {"s1": (0, 1), "s2": (2, 3), "o": (4, 5), "g": (6, 7)}
SIGNALS = [f"{r}_{s}" for r in RINGS for s in ("filled", "taken_act", "taken_dve")] + [
    "ln_ready",
    "split_ready",
    "zoned",
    "weighed",
    "r_ready",
    "router_in",
    "router_exp",
    "wts_ready",
    "var_ready",
    "rstd_ready",
    "out_ready",
    "dve_step"]

PROJ = ["L0q", "L0k", "L0v", "L0o", "L1q", "L1k", "L1v", "L1o", "L2q1", "L2k1", "L2v1", "L2q2", "L2k2",
        "L2v2", "L3q", "L3qs", "L3k", "L3ks", "L3v", "L3o"] + [f"E{m}{e}" for e in range(NE) for m in "qkvo"]
COLS = ["L0q", "L0k", "L1q", "L1k", "L3q", "L3qs", "L3k", "L3ks"] + [f"E{m}{e}" for e in range(NE) for m in "qk"] \
    + [f"f1{c}" for c in range(CH)] + [f"b1{e}{c}" for e in range(NE) for c in range(CH)]
ROWS = ["L0v", "L0o", "L1v", "L1o", "L2v1", "L2v2", "L3v", "L3o", "g1", "be1", "g2", "be2", "g3", "be3",
        "bf2"] + [f"Ev{e}" for e in range(NE)]


def tail_steps(att, out, norm):
    part = {"att": att, "out": out, "norm": norm}
    return {n: [lambda name=name: part[name[:-1]](int(name[-1])) for name in names] for n, names in TAIL.items()}


def build(nc, A, out, totals):
    with ExitStack() as ctx:
        def sb(name, shape, dt=F32):
            return ctx.enter_context(nc.sbuf_tensor(name, shape, dt))

        sem = {n: ctx.enter_context(nc.semaphore(n)) for n in SIGNALS}
        weights_in = ctx.enter_context(nc.semaphore("weights_in"))
        ffn_weights_in = ctx.enter_context(nc.semaphore("ffn_weights_in"))
        x_in = ctx.enter_context(nc.semaphore("x_in"))
        stored = ctx.enter_context(nc.semaphore("stored"))
        consts_set = ctx.enter_context(nc.semaphore("consts_set"))
        bank = [ctx.enter_context(nc.psum_tensor(f"bank{i}", [P, 512], F32)) for i in range(8)]

        wproj = sb("wproj", [P, len(PROJ), P])
        wf = {n: sb(n, [P, s]) for n, s in (("w1_0", NE * 512), ("w2_0", NE * CH * P), ("w1_1", NE * 512),
                                           ("w2_1", NE * CH * P), ("gate_3", NE * 256), ("up_3", NE * 256),
                                           ("down_3", NE * CH3 * P), ("wf1", 512), ("wf2", CH * P))}
        router = sb("router", [P, 3, NE])
        rw1 = sb("rw1", [P, P // 2])
        rw2 = sb("rw2", [P // 2, NE])
        cols = sb("cols", [P, len(COLS)])
        rows = sb("rows", [P, len(ROWS), P])
        rrow = sb("rrow", [P, 3, P // 2])
        rb2 = sb("rb2", [P, NE])
        ebias = sb("ebias", [NE, 2, P])
        rope = sb("rope", [P, 2, P])
        ident = sb("ident", [P, P])
        identb = sb("identb", [P, 2, P], BF16)
        masks = sb("masks", [P, 4, P], BF16)
        band = sb("band", [P, HB])
        tri = sb("tri", [P, NE, NE])

        x_tok = sb("x_tok", [P, NB, P])
        out_tok = sb("out_tok", [P, NB, P])
        h_tok = sb("h_tok", [P, NB, P])
        hh_tok = out_tok
        ctxT = sb("ctxT", [P, NT])
        hT = sb("hT", [P, NT])
        stats = sb("stats", [P, NB, 6])
        mv = sb("mv", [P, NB, 2])
        rstd = sb("rstd", [P, NB])
        power = sb("power", [P, NB])
        vare = sb("vare", [P, NB])
        pad = sb("pad", [P, 1])
        hid = sb("hid", [P, 2, CH, NT])
        x_st = hid[:, 0, CH3, :].rearrange("p (b f) -> p b f", b=NB)
        c_st = hid[:, 1, CH3, :].rearrange("p (b f) -> p b f", b=NB)
        sg = sb("sg", [P, 2, NT])
        qs = sb("qs", [P, NT])
        ks = sb("ks", [P, NT])
        spare = hid[:].rearrange("p a c n -> p (a c n)")
        qf = [sb("qf", [P, NT])[:], spare[:, 0:NT]]
        kf = [sb("kf", [P, NT])[:], spare[:, NT:2 * NT]]
        qm = [sb("qm", [P, HB, NT])[:], spare[:, 2 * NT:6 * NT].rearrange("p (i n) -> p i n", i=HB)]
        km = [sb("km", [P, HB, NT], BF16)[:],
              spare[:, 6 * NT:8 * NT].bitcast(BF16).rearrange("p (i n) -> p i n", i=HB)]
        qb = [sb("qb", [P, NT], BF16)[:], sg[:, 1, 0:NT // 2].bitcast(BF16)]
        kz = sb("kz", [P, 2, BANDS, P])
        qz = sb("qz", [P, 2, BANDS, P], BF16)
        vaug = sb("vaug", [P, 2, NB, H, D + 1])
        oT = [qs, ks]
        mx = sb("mx", [P, NB, H], BF16)
        ex = sb("ex", [P, 2, HB, P])
        rden = sb("rden", [P, NB, H])
        att_tok = sb("att_tok", [P, NB, P])
        attT = sb("attT", [P, NT])
        logit = sb("logit", [P, NB, NE])
        lmax = sb("lmax", [P, NB])
        cmp1, cmp2 = (out_tok[:, 2 * n:2 * n + 2, :].rearrange("p i q -> p (i q)")
                      .rearrange("p (b e f) -> p b e f", b=NB, e=NE) for n in range(2))
        kswap = h_tok[:].rearrange("p b f -> p (b f)")
        top = sb("top", [P, NB, NE])
        lex = sb("lex", [P, NB, NE])
        wts = sb("wts", [P, NB, NE])
        wtsT = attT[0:NE, :]
        lsum = sb("lsum", [P, NB])
        r_full = sg[:, 0, :].rearrange("p (b f) -> p b f", b=NB)
        r_tok = r_full[:, :, 0:P // 2]
        rT = attT[0:P // 2, :]

        loads = [(wproj, A["wproj"]), (router, A["router"]), (rw1, A["rw1"]), (rw2, A["rw2"]), (cols, A["cols"]),
                 (rope, A["rope"]), (ident, A["ident"]),
                 (band, A["band"]), (ebias, A["ebias"])]
        spread = [(rows, A["rows"]), (rrow, A["rrow"]), (rb2, A["rb2"]), (tri, A["tri"])]
        masks_f32 = hid[:, 0, 0, :].rearrange("p (m k) -> p m k", m=4)
        n_loads = len(loads) + len(spread) + 1

        x_dram = A["x"].rearrange("(g b) t f -> g t b f", b=NB)
        c_dram = A["ctx"].rearrange("(g b) t f -> g t b f", b=NB)
        o_dram = out.rearrange("(g b) t f -> g t b f", b=NB)

        def W(name):
            return wproj[:, PROJ.index(name), :]

        def col(name):
            return cols[:, COLS.index(name):COLS.index(name) + 1]

        def over_seqs(ap):
            return ap.unsqueeze(1).to_broadcast([P, NB, ap.shape[1]])

        def row(name):
            return over_seqs(rows[:, ROWS.index(name), :])

        def b4(ap):
            return ap.rearrange("p (b t) -> p b t", b=NB)

        block = ctx.enter_context(nc.Block())
        counted = {}

        @block.sync
        def _(sp):
            def load_group(g):
                sp.dma_start(x_st, x_dram[g]).then_inc(x_in, 16)
                sp.dma_start(c_st, c_dram[g]).then_inc(x_in, 16)

            load_group(0)
            for dst, src in loads:
                sp.dma_start(dst[:], src).then_inc(weights_in, 16)
            sp.dma_start(masks_f32, A["masks"]).then_inc(weights_in, 16)
            for dst, src in spread:
                sp.dma_start(dst[:], src.unsqueeze(0).to_broadcast(list(dst.shape))).then_inc(weights_in, 16)
            for n in wf:
                sp.dma_start(wf[n][:], A[n]).then_inc(ffn_weights_in, 16)
            with sp.Fori(0, GROUPS - 1) as g:
                sp.wait_ge(sem["ln_ready"], g * totals.get("ln_ready", 0) + totals.get("ln_ready", 0))
                load_group(g + 1)

        @block.gpsimd
        def _(pool):
            pool.memset(vaug[:], 1.0).then_inc(consts_set, 1)
            pool.memset(kz[:], 0.0).then_inc(consts_set, 1)
            pool.memset(qz[:], 0.0).then_inc(consts_set, 1)
            pool.memset(power[:], -0.5).then_inc(consts_set, 1)
            pool.memset(vare[:], 1.0).then_inc(consts_set, 1)
            pool.memset(sg[:], 0.0).then_inc(consts_set, 1)
            pool.wait_ge(consts_set, CONSTS)
            with pool.Fori(0, GROUPS) as g:
                t = Tally(totals, g)
                for _ in range(totals.get("var_ready", 0)):
                    pool.wait_ge(sem["var_ready"], t.next("var_ready"))
                    nc.gpsimd.tensor_tensor(rstd[:], vare[:], power[:], ALU.pow).then_inc(sem["rstd_ready"], 1)
                pool.wait_ge(sem["out_ready"], g + 1)
                pool.dma_start(o_dram[g], out_tok[:]).then_inc(stored, 16)
            pool.wait_ge(stored, 16 * GROUPS)

        @block.tensor
        def _(pe):
            pe.wait_ge(weights_in, 16 * n_loads)
            pe.wait_ge(consts_set, CONSTS)
            with pe.Fori(0, GROUPS) as g:
                t = Tally(totals, g)
                ring = {n: Ring(t, n, b) for n, b in RINGS.items()}
                pe.wait_ge(sem["out_ready"], g)

                def open_bank(name, consumer):
                    b, _, taken, old = ring[name].fill(consumer)
                    if old:
                        pe.wait_ge(sem[old[0]], old[1])
                    return bank[b], taken

                def wait_taken(taken):
                    pe.wait_ge(sem[taken[0]], taken[1])

                def to_T(src, ready, rows_=P, wait=True):
                    pe.wait_ge(sem[ready[0]], ready[1])
                    ps, taken = open_bank("g", "act")
                    for b in range(NB):
                        mm = nc.tensor.transpose(ps[0:rows_, b * P:(b + 1) * P], src[:, b, :], ident[:])
                    mm.then_inc(sem["g_filled"], 1)
                    if wait:
                        wait_taken(taken)
                    return taken

                def project(w, src):
                    ps, taken = open_bank("g", "act")
                    nc.tensor.matmul(ps[:], w, src[:], start=True, stop=True).then_inc(sem["g_filled"], 1)
                    return taken

                def by_token(w, src, n, k=P):
                    ps, taken = open_bank("g", "dve")
                    for b in range(NB):
                        mm = nc.tensor.matmul(ps[:, b * n:(b + 1) * n], src[0:k, b * P:(b + 1) * P], w,
                                              start=True, stop=True)
                    mm.then_inc(sem["g_filled"], 1)
                    return taken

                def prepare_q(slot, q, srcT, rot=False):
                    project(W(q), srcT)
                    if rot:
                        project(W(q + "s"), srcT)

                prepare_k = prepare_q

                divided = {}

                def attend(slot, mask, between={}):
                    units = [(b, j) for b in range(NB) for j in range(BANDS)]
                    o_bank, max_taken, exp_taken = {}, {}, {}

                    def scores(b, j):
                        s = slice(b * P, (b + 1) * P)
                        ps, max_taken[b, j] = open_bank("s1", "dve")
                        pe.wait_ge(sem["zoned"], t.next("zoned"))
                        mm = nc.tensor.matmul(ps[:], qz[:, b % 2, j, :], km[slot][:, :, s], start=True, stop=mask is None)
                        if mask is not None:
                            mm = nc.tensor.matmul(ps[:], identb[:, 0, :], masks[:, 2 * mask, :].unsqueeze(1)
                                                  .to_broadcast([P, HB, P]), start=False, stop=True)
                        mm.then_inc(sem["s1_filled"], 1)

                    def scores_t(b, j):
                        s = slice(b * P, (b + 1) * P)
                        ps, exp_taken[b, j] = open_bank("s2", "act")
                        if b == j == 0:
                            pe.wait_ge(sem["split_ready"], t.next("split_ready"))
                        nc.tensor.matmul(ps[:], kz[:, b % 2, j, :], qm[slot][:, :, s], start=True, stop=False)
                        if mask is not None:
                            nc.tensor.matmul(ps[:], identb[:, 0, :], masks[:, 2 * mask + 1, :].unsqueeze(1)
                                             .to_broadcast([P, HB, P]), start=False, stop=False)
                        wait_taken(max_taken[b, j])
                        for i in range(HB):
                            h = HB * j + i
                            mm = nc.tensor.matmul(ps[:, i * P:(i + 1) * P], mx[:, b, h:h + 1].to_broadcast([P, P]),
                                                  identb[:, 1, :], start=False, stop=i == HB - 1)
                        mm.then_inc(sem["s2_filled"], 1)

                    def weigh(n, b, j):
                        if j == 0:
                            o_bank[b] = open_bank("o", "act")
                        wait_taken(exp_taken[b, j])
                        for i in range(HB):
                            mm = nc.tensor.matmul(o_bank[b][0][32 * i:32 * i + D + 1, j * P:(j + 1) * P],
                                                  vaug[:, slot, b, HB * j + i, :], ex[:, n % 2, i, :],
                                                  start=True, stop=True)
                        mm.then_inc(sem["weighed"], 1)

                    def turn(b):
                        wait_taken(o_bank[b][1])
                        ps, taken = open_bank("g", "dve")
                        for j in range(BANDS):
                            mm = nc.tensor.transpose(ps[:, j * P:(j + 1) * P], oT[b % 2][:, j * P:(j + 1) * P], ident[:])
                        mm.then_inc(sem["g_filled"], 1)
                        return taken

                    for n in range(max([STEPS - 1, *between]) + 1):
                        if n < len(units):
                            scores(*units[n])
                        if 1 <= n <= len(units):
                            scores_t(*units[n - 1])
                        if 2 <= n < len(units) + 2:
                            weigh(n - 2, *units[n - 2])
                        for other in between.get(n, []):
                            other()
                        if n in TURNS:
                            taken = divided[TURNS.index(n)] = turn(TURNS.index(n))
                    return taken

                def attention(q, k, v, srcT, kvT, mask, between, rot=False):
                    prepare_q(0, q, srcT, rot)
                    prepare_k(0, k, kvT, rot)
                    by_token(W(v), kvT, P)
                    return attend(0, mask, between)

                def tail(w):
                    last = {}

                    def att(b):
                        pe.wait_ge(sem[divided[b][0]], divided[b][1])
                        ps, last["att"] = open_bank("g", "act")
                        nc.tensor.transpose(ps[:, 0:P], att_tok[:, b, :], ident[:]).then_inc(sem["g_filled"], 1)

                    def out(b):
                        wait_taken(last["att"])
                        ps, _ = open_bank("g", "dve")
                        nc.tensor.matmul(ps[:, 0:P], attT[:, b * P:(b + 1) * P], w, start=True, stop=True)\
                            .then_inc(sem["g_filled"], 1)

                    def norm(b):
                        pe.wait_ge(sem["ln_ready"], t.next("ln_ready"))
                        ps, taken = open_bank("g", "act")
                        nc.tensor.transpose(ps[:, 0:P], h_tok[:, b, :], ident[:]).then_inc(sem["g_filled"], 1)
                        if b == NB - 1:
                            wait_taken(taken)
                    return tail_steps(att, out, norm)

                def out_proj(w, attended):
                    to_T(att_tok, attended)
                    by_token(w, attT, P)

                def experts(w1, w2, chunks, kinds):
                    taken = {}

                    def first(e):
                        for c in range(chunks):
                            for w, who in zip(w1, kinds):
                                ps, taken[e] = open_bank("s1", who)
                                at = (e * chunks + c) * P
                                nc.tensor.matmul(ps[:], w[:, at:at + P], hT[:], start=True, stop=True)\
                                    .then_inc(sem["s1_filled"], 1)

                    def second(e):
                        wait_taken(taken[e])
                        ps, _ = open_bank("s2", "dve")
                        for b in range(NB):
                            for c in range(chunks):
                                at = (e * chunks + c) * P
                                mm = nc.tensor.matmul(ps[:, b * P:(b + 1) * P], hid[:, e % 2, c, b * P:(b + 1) * P],
                                                      w2[:, at:at + P], start=c == 0, stop=c == chunks - 1)
                        mm.then_inc(sem["s2_filled"], 1)
                    return first, second

                def mixture(w1, w2, chunks, kinds):
                    first, second = experts(w1, w2, chunks, kinds)
                    for e in range(NE + 1):
                        if e < NE:
                            first(e)
                        if e:
                            second(e - 1)

                def expert_biases(k):
                    to_T(wts, ("wts_ready", t.next("wts_ready")), NE)
                    by_token(ebias[:, k, :], wtsT, P, NE)

                def to_hT():
                    to_T(h_tok, ("ln_ready", t.next("ln_ready")))

                pe.wait_ge(x_in, g * 32 + 32)
                ps, taken = open_bank("g", "act")
                for b in range(NB):
                    mm = nc.tensor.transpose(ps[:, b * P:(b + 1) * P], c_st[:, b, :], ident[:])
                mm.then_inc(sem["g_filled"], 1)
                wait_taken(taken)
                to_hT()
                attention("L0q", "L0k", "L0v", hT, ctxT, 0, tail(W("L0o")))
                by_token(router[:, 0, :], hT, NE)
                pe.wait_ge(ffn_weights_in, 16 * len(wf))
                mixture([wf["w1_0"]], wf["w2_0"], CH, ["act"])
                to_hT()
                attention("L1q", "L1k", "L1v", hT, ctxT, None, tail(W("L1o")))
                by_token(router[:, 1, :], hT, NE)
                mixture([wf["w1_1"]], wf["w2_1"], CH, ["act"])
                expert_biases(0)
                to_hT()
                prepare_q(0, "L2q1", hT)
                prepare_k(0, "L2k1", hT)
                by_token(W("L2v1"), hT, P)
                attend(0, 0, {4: [lambda: prepare_k(1, "L2k2", ctxT)], 5: [lambda: by_token(W("L2v2"), ctxT, P)]})
                to_hT()
                prepare_q(1, "L2q2", hT)
                attend(1, None)
                to_hT()
                first, second = experts([wf["wf1"]], wf["wf2"], CH, ["act"])
                first(0)
                second(0)
                to_hT()
                by_token(rw1[:], hT, P // 2)
                prepare_q(0, "Eq0", hT)
                prepare_k(0, "Ek0", hT)
                by_token(W("Ev0"), hT, P)
                attended, turned = None, None

                def turn_last():
                    nonlocal turned
                    turned = to_T(att_tok, attended, wait=False)

                def turn_router():
                    nonlocal turned
                    turned = to_T(r_full, ("r_ready", t.next("r_ready")), wait=False)

                for e in range(NE):
                    between = {}
                    if e:
                        between[1] = [turn_last]
                        between[3] = [lambda: (wait_taken(turned), by_token(W(f"Eo{e - 1}"), attT, P))]
                    if e + 1 < NE:
                        between[4] = [lambda: prepare_q((e + 1) % 2, f"Eq{e + 1}", hT)]
                        between[5] = [lambda: prepare_k((e + 1) % 2, f"Ek{e + 1}", hT)]
                        between[6] = [lambda: by_token(W(f"Ev{e + 1}"), hT, P)]
                    else:
                        between[4] = [lambda: prepare_k(0, "L3k", ctxT, True)]
                        between[6] = [lambda: by_token(W("L3v"), ctxT, P)]
                    if e == 0:
                        between[7] = [lambda: turn_router()]
                        between[9] = [lambda: (wait_taken(turned), by_token(rw2[:], rT, NE, P // 2))]
                    attended = attend(e % 2, None, between)
                out_proj(W(f"Eo{NE - 1}"), attended)
                expert_biases(1)
                to_hT()
                prepare_q(0, "L3q", hT, True)
                attend(0, 1, tail(W("L3o")))
                by_token(router[:, 2, :], hT, NE)
                mixture([wf["gate_3"], wf["up_3"]], wf["down_3"], CH3, ["act", "dve"])
            counted["pe"] = (t, ring)

        @block.scalar
        def _(act):
            act.wait_ge(weights_in, 16 * n_loads)
            act.wait_ge(consts_set, CONSTS)
            with act.Fori(0, GROUPS) as g:
                t = Tally(totals, g)
                ring = {n: Ring(t, n, b) for n, b in RINGS.items()}

                def take(name):
                    b, full, _, _ = ring[name].fill("act")
                    act.wait_ge(sem[name + "_filled"], full)
                    return bank[b]

                def skip(name, n=1):
                    for _ in range(n):
                        taken = ring[name].fill("dve")[2]
                    return taken

                def evacuate(dst, parts=P):
                    ps = take("g")
                    nc.scalar.activation(dst, ps[0:parts, :], ACT.Copy).then_inc(sem["g_taken_act"], 1)

                def prepare(slot, dsts, name, bias):
                    ps = take("g")
                    for dst in dsts:
                        if bias:
                            ins = nc.scalar.activation(dst, ps[:], ACT.Identity, bias=col(name))
                        else:
                            ins = nc.scalar.activation(dst, ps[:], ACT.Copy)
                    ins.then_inc(sem["g_taken_act"], 1)

                def prepare_q(slot, name, bias, rot=False):
                    prepare(slot, [qf[slot]] if rot else [qb[slot], qf[slot]], name, bias)
                    if rot:
                        prepare(slot, [qs[:]], name + "s", bias)

                def prepare_k(slot, name, bias, rot=False):
                    prepare(slot, [kf[slot]], name, bias)
                    if rot:
                        prepare(slot, [kswap], name + "s", bias)

                def attend(between={}):
                    for n in range(max([STEPS - 1, *between]) + 1):
                        if 1 <= n <= NB * BANDS:
                            skip("s1")
                            ps = take("s2")
                            before = t.n.get("weighed", 0)
                            if before >= 2:
                                act.wait_ge(sem["weighed"], t.at("weighed", before - 1))
                            t.next("weighed")
                            ins = nc.scalar.activation(ex[:, (n - 1) % 2, :, :],
                                                       ps[:].rearrange("p (i q) -> p i q", i=HB),
                                                       ACT.Exp, scale=SCALE)
                            ins.then_inc(sem["s2_taken_act"], 1)
                        for other in between.get(n, []):
                            other()
                        if n + 1 in TURNS:
                            b = TURNS.index(n + 1)
                            b_, _, taken, _ = ring["o"].fill("act")
                            done = t.n["weighed"] - min(n, NB * BANDS) + BANDS * (b + 1)
                            act.wait_ge(sem["weighed"], t.at("weighed", done))
                            if b >= 2:
                                act.wait_ge(sem[turned[b - 2][0]], turned[b - 2][1])
                            nc.scalar.activation(oT[b % 2][:], bank[b_][:], ACT.Copy).then_inc(sem[taken[0]], 1)
                        if n in TURNS:
                            b = TURNS.index(n)
                            if b == 0:
                                turned = {}
                            turned[b] = skip("g")

                def tail():
                    def att(b):
                        ps = take("g")
                        nc.scalar.activation(attT[:, b * P:(b + 1) * P], ps[:, 0:P], ACT.Copy)\
                            .then_inc(sem["g_taken_act"], 1)

                    def out(b):
                        skip("g")

                    def norm(b):
                        ps = take("g")
                        nc.scalar.activation(hT[:, b * P:(b + 1) * P], ps[:, 0:P], ACT.Copy)\
                            .then_inc(sem["g_taken_act"], 1)
                    return tail_steps(att, out, norm)

                def attention(bias, q, k, rot=False):
                    prepare_q(0, q, bias, rot)
                    prepare_k(0, k, bias, rot)
                    skip("g")
                    attend(tail())

                def out_proj():
                    evacuate(attT[:])
                    skip("g")

                def gates(times=1):
                    skip("g")
                    for _ in range(times):
                        act.wait_ge(sem["router_in"], t.next("router_in"))
                        nc.scalar.activation(lex[:], logit[:], ACT.Exp)\
                            .then_inc(sem["router_exp"], 1)

                def mixture(func, ne, biases=None, routed=lambda: None):
                    for e in range(ne):
                        for c in range(CH):
                            ps = take("s1")
                            kw = {"bias": col(biases(e, c))} if biases else {}
                            ins = nc.scalar.activation(hid[:, e % 2, c, :], ps[:], func, **kw)
                            ins.then_inc(sem["s1_taken_act"], 1)
                        if e == 0:
                            routed()
                        skip("s2")

                def expert_biases():
                    evacuate(wtsT, NE)
                    skip("g")

                evacuate(ctxT[:])
                evacuate(hT[:])
                attention(True, "L0q", "L0k")
                mixture(ACT.Relu, NE, routed=gates)
                evacuate(hT[:])
                attention(True, "L1q", "L1k")
                gates()
                mixture(ACT.Gelu, NE, lambda e, c: f"b1{e}{c}")
                expert_biases()
                evacuate(hT[:])
                prepare_q(0, "L2q1", False)
                prepare_k(0, "L2k1", False)
                skip("g")
                attend({5: [lambda: prepare_k(1, "L2k2", False)], 6: [lambda: skip("g")]})
                evacuate(hT[:])
                prepare_q(1, "L2q2", False)
                attend()
                evacuate(hT[:])
                mixture(ACT.Relu, 1, lambda e, c: f"f1{c}")
                evacuate(hT[:])
                skip("g")
                prepare_q(0, "Eq0", True)
                prepare_k(0, "Ek0", True)
                skip("g")
                for e in range(NE):
                    between = {}
                    if e:
                        between[2] = [lambda: evacuate(attT[:])]
                        between[3] = [lambda: skip("g")]
                    if e + 1 < NE:
                        between[5] = [lambda: prepare_q((e + 1) % 2, f"Eq{e + 1}", True)]
                        between[6] = [lambda: prepare_k((e + 1) % 2, f"Ek{e + 1}", True), lambda: skip("g")]
                    else:
                        between[5] = [lambda: prepare_k(0, "L3k", True, True)]
                        between[7] = [lambda: skip("g")]
                    if e == 0:
                        between[8] = [lambda: evacuate(rT, P // 2)]
                        between[11] = [lambda: gates()]
                    attend(between)
                out_proj()
                expert_biases()
                evacuate(hT[:])
                prepare_q(0, "L3q", True, True)
                attend(tail())
                gates(2)
                multiplied = []
                for e in range(NE):
                    for c in range(CH3):
                        ps = take("s1")
                        multiplied.append(ring["s1"].fill("dve")[2])
                        n = e * CH3 + c
                        if n >= 2:
                            act.wait_ge(sem[multiplied[n - 2][0]], multiplied[n - 2][1])
                        nc.scalar.activation(sg[:, n % 2, :], ps[:], ACT.Silu).then_inc(sem["s1_taken_act"], 1)
                    skip("s2")
            counted["act"] = (t, ring)

        @block.vector
        def _(dve):
            dve.wait_ge(weights_in, 16 * n_loads)
            nc.vector.memset(bank[RINGS["o"][0]][:], 0.0).then_inc(consts_set, 1)
            nc.vector.memset(bank[RINGS["o"][1]][:], 0.0).then_inc(consts_set, 1)
            nc.vector.tensor_copy(masks[:], masks_f32).then_inc(consts_set, 1)
            nc.vector.tensor_copy(identb[:, 0, :], ident[:]).then_inc(consts_set, 1)
            nc.vector.tensor_scalar(identb[:, 1, :], ident[:], -1.0, None, ALU.mult).then_inc(consts_set, 1)
            dve.wait_ge(consts_set, CONSTS)
            with dve.Fori(0, GROUPS) as g:
                t = Tally(totals, g)
                ring = {n: Ring(t, n, b) for n, b in RINGS.items()}

                def settle(ins, name="dve_step"):
                    ins.then_inc(sem[name], 1)
                    dve.wait_ge(sem[name], t.next(name))

                def settle_taken(ins, taken):
                    ins.then_inc(sem[taken[0]], 1)
                    dve.wait_ge(sem[taken[0]], taken[1])

                def take(name):
                    b, full, taken, _ = ring[name].fill("dve")
                    dve.wait_ge(sem[name + "_filled"], full)
                    return bank[b], taken

                def skip(name, n=1):
                    for _ in range(n):
                        taken = ring[name].fill("act")[2]
                    return taken

                def normalize(src, dst, gain=None, shift=None, relu=False, seqs=range(NB)):
                    for b in seqs:
                        ins = nc.vector.bn_stats(stats[:, b, :], src[:, b, :])
                    settle(ins)
                    nc.vector.memset(pad[:], 0.0)
                    for b in seqs:
                        ins = nc.vector.bn_aggr(mv[:, b, :], stats[:, b, :])
                    settle(ins)
                    own = slice(seqs[0], seqs[-1] + 1)
                    nc.vector.tensor_scalar(vare[:, own], mv[:, own, 1], EPS, None, ALU.add)\
                        .then_inc(sem["var_ready"], 1)
                    t.next("var_ready")
                    dve.wait_ge(sem["rstd_ready"], t.next("rstd_ready"))
                    for b in seqs:
                        ins = nc.vector.tensor_scalar(dst[:, b, :], src[:, b, :], mv[:, b, 0:1], rstd[:, b:b + 1],
                                                      ALU.subtract, ALU.mult)
                    if gain is not None:
                        settle(ins)
                        settle(nc.vector.tensor_tensor(dst[:], dst[:], gain, ALU.mult))
                        ins = nc.vector.tensor_tensor(dst[:], dst[:], shift, ALU.add)
                        if relu:
                            settle(ins)
                            ins = nc.vector.tensor_scalar(dst[:], dst[:], 0.0, None, ALU.max)
                    return ins

                def norm_to_hT(src, **kw):
                    settle(normalize(src, h_tok, **kw), "ln_ready")
                    skip("g")

                def values(slot, v):
                    ps, taken = take("g")
                    for b in range(NB):
                        ins = nc.vector.tensor_tensor(vaug[:, slot, b, :, 0:D],
                                                      ps[:, b * P:(b + 1) * P].rearrange("p (h d) -> p h d", d=D),
                                                      rows[:, ROWS.index(v), :].rearrange("p (h d) -> p h d", d=D),
                                                      ALU.add)
                    ins.then_inc(sem[taken[0]], 1)

                def split_k(slot, projected, heads=range(HB)):
                    dve.wait_ge(sem[projected[0]], projected[1])
                    for i in heads:
                        ins = nc.vector.tensor_scalar(km[slot][:, i, :], kf[slot], band[:, i:i + 1], None, ALU.mult)
                    return ins

                def split_q(slot, heads=range(HB)):
                    for i in heads:
                        ins = nc.vector.tensor_scalar(qm[slot][:, i, :], qf[slot], band[:, i:i + 1], None, ALU.mult)
                    return ins

                def rotate(projected, a, s):
                    dve.wait_ge(sem[projected[0]], projected[1])
                    nc.vector.tensor_tensor(b4(a), b4(a), over_seqs(rope[:, 0, :]), ALU.mult)
                    settle(nc.vector.tensor_tensor(b4(s), b4(s), over_seqs(rope[:, 1, :]), ALU.mult))
                    settle(nc.vector.tensor_tensor(a, a, s, ALU.add))

                def attend(slot=0, between={}, late_q=True):
                    def zone(b, j):
                        p, s = slice(32 * j, 32 * j + 32), slice(b * P, (b + 1) * P)
                        nc.vector.tensor_copy(qz[p, b % 2, j, :], qb[slot][p, s])
                        nc.vector.tensor_copy(kz[p, b % 2, j, :], kf[slot][p, s]).then_inc(sem["zoned"], 1)

                    def maximum(b, j):
                        ps, taken = take("s1")
                        ins = nc.vector.tensor_reduce(mx[:, b, HB * j:HB * j + HB],
                                                      ps[:].rearrange("p (i k) -> p i k", i=HB), AX.X, ALU.max)
                        ins.then_inc(sem[taken[0]], 1)
                        skip("s2")

                    def divide(b):
                        ps, taken = take("g")
                        o = ps[:].rearrange("p (h d) -> p h d", d=32)
                        settle(nc.vector.reciprocal(rden[:, b, :], o[:, :, D]))
                        ins = nc.vector.tensor_tensor(att_tok[:, b, :].rearrange("p (h d) -> p h d", d=D),
                                                      o[:, :, 0:D],
                                                      rden[:, b, :].unsqueeze(2).to_broadcast([P, H, D]), ALU.mult)
                        ins.then_inc(sem[taken[0]], 1)
                        return taken

                    for n in range(LEAD):
                        zone(n // BANDS, n % BANDS)
                    if late_q:
                        split_q(slot).then_inc(sem["split_ready"], 1)
                    for n in range(max([STEPS - 1, *between]) + 1):
                        if n + LEAD < NB * BANDS:
                            zone((n + LEAD) // BANDS, (n + LEAD) % BANDS)
                        if n < NB * BANDS:
                            maximum(n // BANDS, n % BANDS)
                        for other in between.get(n, []):
                            other()
                        if n in TURNS:
                            taken = divide(TURNS.index(n))
                    dve.wait_ge(sem[taken[0]], taken[1])

                def attention(v, between):
                    projected = skip("g", 2)
                    values(0, v)
                    split_k(0, projected)
                    attend(0, between)

                def out_proj():
                    skip("g")
                    return take("g")

                def tail(bias):
                    def att(b):
                        skip("g")

                    def out(b):
                        ps, taken = take("g")
                        settle_taken(nc.vector.tensor_tensor(x_tok[:, b, :], x_tok[:, b, :], ps[:, 0:P], ALU.add),
                                     taken)
                        settle(nc.vector.tensor_tensor(x_tok[:, b, :], x_tok[:, b, :],
                                                       rows[:, ROWS.index(bias), :], ALU.add))
                        settle(normalize(x_tok, h_tok, seqs=[b]), "ln_ready")

                    def norm(b):
                        skip("g")
                    return tail_steps(att, out, norm)

                def gates(bias=False, twice=False):
                    ps, taken = take("g")
                    lg = ps[:, 0:NB * NE].rearrange("p (b e) -> p b e", b=NB)
                    if bias:
                        ins = nc.vector.tensor_tensor(logit[:], lg, over_seqs(rb2[:]), ALU.add)
                    else:
                        ins = nc.vector.tensor_copy(logit[:], lg)
                    settle_taken(ins, taken)
                    nc.vector.tensor_reduce(lmax[:], logit[:], AX.X, ALU.max)
                    for b in range(NB):
                        other = logit[:, b, :].unsqueeze(1).to_broadcast([P, NE, NE])
                        own = logit[:, b, :].unsqueeze(2).to_broadcast([P, NE, NE])
                        nc.vector.tensor_tensor(cmp1[:, b], other, own, ALU.is_gt)
                        ins = nc.vector.tensor_tensor(cmp2[:, b], other, own, ALU.is_equal)
                    settle(ins)
                    settle(nc.vector.tensor_tensor(cmp2, cmp2, tri[:].unsqueeze(1)
                                                   .to_broadcast([P, NB, NE, NE]), ALU.mult))
                    settle(nc.vector.tensor_tensor(cmp1, cmp1, cmp2, ALU.add))
                    settle(nc.vector.tensor_reduce(top[:], cmp1, AX.X, ALU.add))
                    nc.vector.tensor_scalar(top[:], top[:], 1.5, None, ALU.is_lt)
                    ins = nc.vector.tensor_tensor(logit[:], logit[:], lmax[:].unsqueeze(2).to_broadcast([P, NB, NE]),
                                                  ALU.subtract)
                    ins.then_inc(sem["router_in"], 1)
                    t.next("router_in")

                    def exped():
                        dve.wait_ge(sem["router_exp"], t.next("router_exp"))

                    def share(dst):
                        settle(nc.vector.tensor_reduce(lsum[:], dst[:], AX.X, ALU.add))
                        settle(nc.vector.reciprocal(lsum[:], lsum[:]))
                        return nc.vector.tensor_tensor(dst[:], dst[:], lsum[:].unsqueeze(2)
                                                       .to_broadcast([P, NB, NE]), ALU.mult)
                    exped()
                    if twice:
                        settle(share(lex))
                        ins = nc.vector.tensor_tensor(logit[:], lex[:], lsum[:].unsqueeze(2)
                                                      .to_broadcast([P, NB, NE]), ALU.subtract)
                        ins.then_inc(sem["router_in"], 1)
                        t.next("router_in")
                        exped()
                    settle(nc.vector.tensor_tensor(wts[:], lex[:], top[:], ALU.mult))
                    return share(wts)

                def add_weighted(took, e):
                    ps, taken = took
                    for b in range(NB):
                        ins = nc.vector.scalar_tensor_tensor(x_tok[:, b, :], ps[:, b * P:(b + 1) * P],
                                                             wts[:, b, e:e + 1], x_tok[:, b, :], ALU.mult, ALU.add)
                    settle_taken(ins, taken)

                def expert_biases():
                    skip("g")
                    ps, taken = take("g")
                    settle_taken(nc.vector.tensor_tensor(x_tok[:], x_tok[:], b4(ps[:]), ALU.add), taken)

                def mixture():
                    for e in range(NE):
                        skip("s1", CH)
                        add_weighted(take("s2"), e)

                dve.wait_ge(x_in, g * 32 + 32)
                dve.wait_ge(stored, g * 16)
                settle(nc.vector.tensor_copy(x_tok[:], x_st))
                skip("g")
                norm_to_hT(x_tok)
                attention("L0v", tail("L0o"))
                settle(gates())
                mixture()
                norm_to_hT(x_tok)
                attention("L1v", tail("L1o"))
                settle(gates(), "wts_ready")
                mixture()
                expert_biases()
                norm_to_hT(x_tok)
                projected = skip("g", 2)
                values(0, "L2v1")
                split_k(0, projected)
                ctx_k = []
                attend(0, {5: [lambda: ctx_k.append(skip("g"))], 6: [lambda: values(1, "L2v2")],
                           9: [lambda: split_k(1, ctx_k[0], [0, 1])], 10: [lambda: split_k(1, ctx_k[0], [2, 3])]})
                settle(nc.vector.tensor_tensor(hh_tok[:], h_tok[:], att_tok[:], ALU.add))
                norm_to_hT(hh_tok, gain=row("g1"), shift=row("be1"))
                projected = skip("g")
                dve.wait_ge(sem[projected[0]], projected[1])
                attend(1)
                settle(nc.vector.tensor_tensor(hh_tok[:], h_tok[:], att_tok[:], ALU.add))
                norm_to_hT(hh_tok, gain=row("g2"), shift=row("be2"))
                skip("s1", CH)
                ps, taken = take("s2")
                settle_taken(nc.vector.tensor_tensor(hh_tok[:], h_tok[:], b4(ps[:]), ALU.add), taken)
                settle(nc.vector.tensor_tensor(hh_tok[:], hh_tok[:], row("bf2"), ALU.add))
                settle(normalize(hh_tok, h_tok, gain=row("g3"), shift=row("be3")))
                settle(nc.vector.tensor_tensor(x_tok[:], x_tok[:], h_tok[:], ALU.add))
                norm_to_hT(x_tok)
                ps, taken = take("g")
                ins = nc.vector.tensor_tensor(r_tok, ps[:, 0:NB * P // 2].rearrange("p (b f) -> p b f", b=NB),
                                              over_seqs(rrow[:, 0, :]), ALU.add)
                settle_taken(ins, taken)

                def router_hidden():
                    normalize(r_tok, r_tok, gain=over_seqs(rrow[:, 1, :]), shift=over_seqs(rrow[:, 2, :]), relu=True)\
                        .then_inc(sem["r_ready"], 1)
                    t.next("r_ready")

                projected = skip("g", 2)
                values(0, "Ev0")
                split_k(0, projected)
                for e in range(NE):
                    between = {}
                    if e:
                        between[2] = [lambda: skip("g")]
                        between[4] = [lambda: add_weighted(take("g"), e - 1)]
                    if e + 1 < NE:
                        slot = (e + 1) % 2
                        projected = []
                        between[6] = [lambda: projected.append(skip("g", 2))]
                        between[7] = [lambda: values(slot, f"Ev{e + 1}")]
                        for i in range(HB):
                            between.setdefault(9 + i, []).append(lambda i=i: split_k(slot, projected[0], [i]))
                        for i in range(HB - 1):
                            between[13 + i] = [lambda i=i: split_q(slot, [i])]
                        between[12 + HB] = [lambda: split_q(slot, [HB - 1]).then_inc(sem["split_ready"], 1)]
                    else:
                        ks_projected = []
                        between[6] = [lambda: ks_projected.append(skip("g", 2))]
                        between[7] = [lambda: values(0, "L3v")]
                        between[10] = [lambda: rotate(ks_projected[0], kf[0], kswap)]
                        for i in range(HB):
                            between[12 + i] = [lambda i=i: split_k(0, ks_projected[0], [i])]
                    if e == 0:
                        between.setdefault(2, []).append(router_hidden)
                        between.setdefault(8, []).append(lambda: skip("g"))
                        between[11].append(lambda: settle(gates(bias=True), "wts_ready"))
                    attend(e % 2, between, late_q=e == 0)
                add_weighted(out_proj(), NE - 1)
                expert_biases()
                norm_to_hT(x_tok)
                projected = skip("g", 2)
                rotate(projected, qf[0], qs[:])
                settle(nc.vector.tensor_copy(qb[0], qf[0]))
                attend(0, tail("L3o"))
                settle(gates(twice=True))

                def gate_hidden(e):
                    for c in range(CH3):
                        n = e * CH3 + c
                        silu = skip("s1")
                        dve.wait_ge(sem[silu[0]], silu[1])
                        ps, taken = take("s1")
                        ins = nc.vector.tensor_tensor(hid[:, e % 2, c, :], ps[:], sg[:, n % 2, :], ALU.mult)
                        ins.then_inc(sem[taken[0]], 1)

                for e in range(NE + 1):
                    if e < NE:
                        gate_hidden(e)
                    if e:
                        add_weighted(take("s2"), e - 1)
                nc.vector.tensor_copy(out_tok[:], x_tok[:]).then_inc(sem["out_ready"], 1)
                dve.wait_ge(sem["out_ready"], t.next("out_ready"))
            counted["dve"] = (t, ring)
    return counted


def totals_of(counted):
    got = {}
    for t, ring in counted.values():
        for name, n in t.n.items():
            got[name] = max(got.get(name, 0), n)
        for r in ring.values():
            assert r.name == "o" or got.get(f"{r.name}_filled", len(r.used)) == len(r.used), r.name
            got[f"{r.name}_filled"] = max(len(r.used), got.get(f"{r.name}_filled", 0))
            for who, n in r.count.items():
                got[f"{r.name}_taken_{who}"] = max(n, got.get(f"{r.name}_taken_{who}", 0))
    return got


def laid_out(i):
    f = {k: np.asarray(v) for k, v in i.items()}

    def heads(w):
        return w.transpose(1, 0, 2).reshape(P, P)

    swap = np.arange(P) ^ (D // 2)
    proj = {
        "L0q": f["L0_xattn_Wq"].T, "L0k": f["L0_xattn_Wk"].T, "L0v": f["L0_xattn_Wv"].T, "L0o": f["L0_xattn_Wo"].T,
        "L1q": f["L1_xattn_Wq"], "L1k": f["L1_xattn_Wk"], "L1v": f["L1_xattn_Wv"], "L1o": f["L1_xattn_Wo"],
        "L2q1": heads(f["L2_xattn_Wq1"]), "L2k1": heads(f["L2_xattn_Wk1"]), "L2v1": heads(f["L2_xattn_Wv1"]),
        "L2q2": heads(f["L2_xattn_Wq2"]), "L2k2": heads(f["L2_xattn_Wk2"]), "L2v2": heads(f["L2_xattn_Wv2"]),
        "L3q": f["L3_xattn_q_w"].T, "L3qs": f["L3_xattn_q_w"].T[:, swap], "L3k": f["L3_xattn_k_w"].T,
        "L3ks": f["L3_xattn_k_w"].T[:, swap], "L3v": f["L3_xattn_v_w"].T, "L3o": f["L3_xattn_o_w"].T}
    for e in range(NE):
        for m in "qkvo":
            proj[f"E{m}{e}"] = f[f"L2_ffn_{m}W"][e].T
    col = {"L0q": f["L0_xattn_bq"], "L0k": f["L0_xattn_bk"], "L1q": f["L1_xattn_bq"], "L1k": f["L1_xattn_bk"],
           "L3q": f["L3_xattn_q_b"], "L3qs": f["L3_xattn_q_b"][swap], "L3k": f["L3_xattn_k_b"],
           "L3ks": f["L3_xattn_k_b"][swap]}
    for e in range(NE):
        col[f"Eq{e}"], col[f"Ek{e}"] = f["L2_ffn_qb"][e], f["L2_ffn_kb"][e]
        for c in range(CH):
            col[f"b1{e}{c}"] = f["L1_ffn_b1"][e, c * P:(c + 1) * P]
    for c in range(CH):
        col[f"f1{c}"] = f["L2_xattn_bf1"][c * P:(c + 1) * P]
    row = {"L0v": f["L0_xattn_bv"], "L0o": f["L0_xattn_bo"], "L1v": f["L1_xattn_bv"], "L1o": f["L1_xattn_bo"],
           "L2v1": f["L2_xattn_bv1"].reshape(P), "L2v2": f["L2_xattn_bv2"].reshape(P), "L3v": f["L3_xattn_v_b"],
           "L3o": f["L3_xattn_o_b"], "bf2": f["L2_xattn_bf2"]}
    for n in "123":
        row["g" + n], row["be" + n] = f["L2_xattn_g" + n], f["L2_xattn_be" + n]
    for e in range(NE):
        row[f"Ev{e}"] = f["L2_ffn_vb"][e]

    def down(w, chunks):
        return w.reshape(-1, chunks, P, P).transpose(2, 0, 1, 3).reshape(P, -1)

    a = {
        "x": f["x"], "ctx": f["ctx_1024"],
        "wproj": np.stack([proj[n] for n in PROJ], 1), "cols": np.stack([col[n] for n in COLS], 1),
        "rows": np.stack([row[n] for n in ROWS], 0),
        "w1_0": f["L0_ffn_w1"].transpose(2, 0, 1).reshape(P, -1), "w2_0": down(f["L0_ffn_w2"].transpose(0, 2, 1), CH),
        "w1_1": f["L1_ffn_W1"].transpose(2, 0, 1).reshape(P, -1), "w2_1": down(f["L1_ffn_W2"].transpose(0, 2, 1), CH),
        "gate_3": f["L3_ffn_kernel_gating_EDF"].transpose(1, 0, 2).reshape(P, -1),
        "up_3": f["L3_ffn_kernel_up_EDF"].transpose(1, 0, 2).reshape(P, -1),
        "down_3": down(f["L3_ffn_kernel_down_EFD"], CH3),
        "wf1": f["L2_xattn_Wf1"], "wf2": down(f["L2_xattn_Wf2"], CH),
        "router": np.stack([f["L0_ffn_gate_w"].T, f["L1_ffn_Wr"].T, f["L3_ffn_router_kernel_DE"]], 1),
        "rw1": f["L2_ffn_rW1"].T, "rw2": f["L2_ffn_rW2"].T,
        "rrow": np.stack([f["L2_ffn_rb1"], f["L2_ffn_ln_g"], f["L2_ffn_ln_b"]], 0), "rb2": f["L2_ffn_rb2"],
        "ebias": np.stack([f["L1_ffn_b2"], f["L2_ffn_ob"]], 1),
    }
    angle = (np.arange(P, dtype=np.float32)[None, :]
             * (1.0 / np.float32(10000.0) ** (np.arange(D // 2, dtype=np.float32) / (D // 2)))[np.arange(P) % (D // 2), None])
    sign = np.where(np.arange(P) % D < D // 2, -1.0, 1.0)[:, None]
    a["rope"] = np.stack([np.cos(angle), np.sin(angle) * sign], 1).astype(np.float32)
    one = np.eye(P, dtype=np.float32)
    a["ident"] = one
    q, k = np.arange(P)[:, None], np.arange(P)[None, :]
    causal, window = k <= q, (k <= q) & (k >= q - WINDOW)
    a["masks"] = np.stack([np.where(m, 0.0, NEG) for m in (causal, causal.T, window, window.T)], 1).astype(np.float32)
    a["band"] = (np.arange(P)[:, None] % 32 // D == np.arange(HB)[None, :]).astype(np.float32)
    a["tri"] = (np.arange(NE)[None, :] < np.arange(NE)[:, None]).astype(np.float32)
    return {n: np.ascontiguousarray(v) for n, v in a.items()}


def kernel(**inputs):
    import concourse.bacc as bacc
    from concourse.bass_utils import run_bass_kernel_spmd as run

    arrays = laid_out(inputs)

    def program(totals):
        nc = bacc.Bacc("TRN2", target_bir_lowering=False, num_devices=1)
        A = {n: nc.dram_tensor(f"in_{n}", a.shape, mybir.dt.from_np(a.dtype), kind="ExternalInput").ap()
             for n, a in arrays.items()}
        out = nc.dram_tensor("out_x", (NSEQ, P, P), F32, kind="ExternalOutput").ap()
        return nc, totals_of(build(nc, A, out, totals))

    _, totals = program({})
    nc, again = program(totals)
    assert again == totals
    r = run(nc, [{f"in_{n}": a for n, a in arrays.items()}], core_ids=[0])
    return r.results[0]["out_x"]
```
